# Optimizing a Trainium2 kernel written in Bass

```python
import numpy as np
import jax
import jax.numpy as jnp

def _softmax(x, axis=-1):
    return jax.nn.softmax(x, axis=axis)

def _gelu(x):
    return jax.nn.gelu(x, approximate=True)

def _silu(x):
    return jax.nn.silu(x)

def _sigmoid(x):
    return jax.nn.sigmoid(x)

def _layernorm(x, axis=-1, eps=1e-05):
    m = jnp.mean(x, axis=axis, keepdims=True)
    v = jnp.var(x, axis=axis, keepdims=True)
    return (x - m) / jnp.sqrt(v + eps)

def _scatter_add(tgt, idx, src, axis=0):
    return tgt.at[idx].add(src)

def _segment_sum(src, seg, n):
    return jax.ops.segment_sum(src, seg, n)
kernel_name = 'mk_decoder_postln_d1_seqx_r8_94738b'

def setup_inputs(seed: int=0):
    np.random.seed(seed)
    _w = jnp.asarray

    def _rec_inputs():
        import jax
        import jax.numpy as jnp
        _rk = jax.random.key(seed)
        x = -0.0002928 + 1 * jax.random.normal(jax.random.fold_in(_rk, 1), (8, 256, 128), jnp.float32)
        _lenS = 256 - jax.random.randint(jax.random.fold_in(_rk, 7), (8,), 0, max(1, 256 // 4) + 1, jnp.int32)
        _lenS2 = 512 - jax.random.randint(jax.random.fold_in(_rk, 8), (8,), 0, max(1, 512 // 4) + 1, jnp.int32)
        _ctx_1024P = jax.random.normal(jax.random.fold_in(_rk, 11), (8, 16, 128), jnp.float32)
        _ctx_1024c = jax.random.dirichlet(jax.random.fold_in(_rk, 511), 0.3 * jnp.ones((16,), jnp.float32), (8, 512))
        _ctx_1024t = jnp.einsum('bsk,bkd->bsd', _ctx_1024c, _ctx_1024P)
        _ctx_1024t = _ctx_1024t * jax.lax.rsqrt(jnp.mean(jnp.square(_ctx_1024t)) + 1e-12) * 0.953939
        ctx_1024 = -1.39393e-06 + 0.999914 * (_ctx_1024t + 0.3 * jax.random.normal(jax.random.fold_in(_rk, 611), (8, 512, 128), jnp.float32))
        return (x, ctx_1024)
    x, ctx_1024 = _rec_inputs()

    def _L0_attn_setup():
        import jax, jax.numpy as jnp
        import numpy as np
        DIM = 128
        NUM_HEADS = 16
        HEAD_DIM = DIM // NUM_HEADS
        key = jax.random.key(seed)
        ks = jax.random.split(key, 9)
        s = 1.0 / np.sqrt(DIM)
        return {'x': jax.random.normal(ks[0], (2, 512, DIM), dtype=jnp.float32), 'Wq': jax.random.normal(ks[1], (DIM, DIM), dtype=jnp.float32) * s, 'bq': jnp.zeros((DIM,), dtype=jnp.float32), 'Wk': jax.random.normal(ks[2], (DIM, DIM), dtype=jnp.float32) * s, 'bk': jnp.zeros((DIM,), dtype=jnp.float32), 'Wv': jax.random.normal(ks[3], (DIM, DIM), dtype=jnp.float32) * s, 'bv': jnp.zeros((DIM,), dtype=jnp.float32), 'Wo': jax.random.normal(ks[4], (DIM, DIM), dtype=jnp.float32) * s, 'bo': jnp.zeros((DIM,), dtype=jnp.float32)}
    _L0_attn_all = _L0_attn_setup()
    _L0_attn_in = {k: v for k, v in _L0_attn_all.items() if k in ('Wq', 'bq', 'Wk', 'bk', 'Wv', 'bv', 'Wo', 'bo')}
    del _L0_attn_all

    def _L0_xattn_setup():
        import jax, jax.numpy as jnp
        import numpy as np
        from math import sqrt
        D_MODEL = 128
        N_HEADS = 16
        E = D_MODEL // N_HEADS
        key = jax.random.key(seed)
        ks = jax.random.split(key, 11)
        B, L, S = (2, 256, 256)
        s = 1.0 / sqrt(D_MODEL)
        return {'queries': jax.random.normal(ks[0], (B, L, D_MODEL), jnp.float32), 'keys': jax.random.normal(ks[1], (B, S, D_MODEL), jnp.float32), 'values': jax.random.normal(ks[2], (B, S, D_MODEL), jnp.float32), 'Wq': jax.random.normal(ks[3], (D_MODEL, D_MODEL), jnp.float32) * s, 'bq': jnp.zeros((D_MODEL,), jnp.float32), 'Wk': jax.random.normal(ks[4], (D_MODEL, D_MODEL), jnp.float32) * s, 'bk': jnp.zeros((D_MODEL,), jnp.float32), 'Wv': jax.random.normal(ks[5], (D_MODEL, D_MODEL), jnp.float32) * s, 'bv': jnp.zeros((D_MODEL,), jnp.float32), 'Wo': jax.random.normal(ks[6], (D_MODEL, D_MODEL), jnp.float32) * s, 'bo': jnp.zeros((D_MODEL,), jnp.float32)}
    _L0_xattn_all = _L0_xattn_setup()
    _L0_xattn_in = {k: v for k, v in _L0_xattn_all.items() if k in ('Wq', 'bq', 'Wk', 'bk', 'Wv', 'bv', 'Wo', 'bo')}
    del _L0_xattn_all

    def _L0_ffn_setup():
        import jax, jax.numpy as jnp
        import numpy as np
        S, B, H, I, E = (64, 2, 128, 352, 8)
        key = jax.random.key(seed)
        ks = jax.random.split(key, 5)
        return {'hidden_states': jax.random.normal(ks[0], (S, B, H), dtype=jnp.float32), 'router_w': jax.random.normal(ks[1], (E, H), dtype=jnp.float32) * 0.02, 'gate_w': jax.random.normal(ks[2], (E, I, H), dtype=jnp.float32) * 0.02, 'up_w': jax.random.normal(ks[3], (E, I, H), dtype=jnp.float32) * 0.02, 'down_w': jax.random.normal(ks[4], (E, H, I), dtype=jnp.float32) * 0.02}
    _L0_ffn_all = _L0_ffn_setup()
    _L0_ffn_in = {k: v for k, v in _L0_ffn_all.items() if k in ('router_w', 'gate_w', 'up_w', 'down_w')}
    del _L0_ffn_all
    return {'x': x, 'ctx_1024': ctx_1024, 'L0_attn_Wq': _L0_attn_in['Wq'], 'L0_attn_bq': _L0_attn_in['bq'], 'L0_attn_Wk': _L0_attn_in['Wk'], 'L0_attn_bk': _L0_attn_in['bk'], 'L0_attn_Wv': _L0_attn_in['Wv'], 'L0_attn_bv': _L0_attn_in['bv'], 'L0_attn_Wo': _L0_attn_in['Wo'], 'L0_attn_bo': _L0_attn_in['bo'], 'L0_xattn_Wq': _L0_xattn_in['Wq'], 'L0_xattn_bq': _L0_xattn_in['bq'], 'L0_xattn_Wk': _L0_xattn_in['Wk'], 'L0_xattn_bk': _L0_xattn_in['bk'], 'L0_xattn_Wv': _L0_xattn_in['Wv'], 'L0_xattn_bv': _L0_xattn_in['bv'], 'L0_xattn_Wo': _L0_xattn_in['Wo'], 'L0_xattn_bo': _L0_xattn_in['bo'], 'L0_ffn_router_w': _L0_ffn_in['router_w'], 'L0_ffn_gate_w': _L0_ffn_in['gate_w'], 'L0_ffn_up_w': _L0_ffn_in['up_w'], 'L0_ffn_down_w': _L0_ffn_in['down_w']}

def reference(x, ctx_1024, L0_attn_Wq, L0_attn_bq, L0_attn_Wk, L0_attn_bk, L0_attn_Wv, L0_attn_bv, L0_attn_Wo, L0_attn_bo, L0_xattn_Wq, L0_xattn_bq, L0_xattn_Wk, L0_xattn_bk, L0_xattn_Wv, L0_xattn_bv, L0_xattn_Wo, L0_xattn_bo, L0_ffn_router_w, L0_ffn_gate_w, L0_ffn_up_w, L0_ffn_down_w):
    import jax
    import jax.numpy as jnp

    def _L0_attn_ref(x, Wq, bq, Wk, bk, Wv, bv, Wo, bo):
        import jax, jax.numpy as jnp
        import numpy as np
        DIM = 128
        NUM_HEADS = 16
        HEAD_DIM = DIM // NUM_HEADS
        q = jnp.einsum('bsd,df->bsf', x, Wq) + bq
        k = jnp.einsum('bsd,df->bsf', x, Wk) + bk
        v = jnp.einsum('bsd,df->bsf', x, Wv) + bv
        scale = 1.0 / np.sqrt(HEAD_DIM)
        scores = jnp.einsum('bqd,bkd->bqk', q, k) * scale
        attn = jax.nn.softmax(scores, axis=-1)
        out = jnp.einsum('bqk,bkd->bqd', attn, v)
        return jnp.einsum('bsd,df->bsf', out, Wo) + bo

    def _L0_xattn_ref(queries, keys, values, Wq, bq, Wk, bk, Wv, bv, Wo, bo):
        import jax, jax.numpy as jnp
        import numpy as np
        from math import sqrt
        D_MODEL = 128
        N_HEADS = 16
        E = D_MODEL // N_HEADS
        B, L, _ = queries.shape
        S = keys.shape[1]
        H = N_HEADS
        q = (queries @ Wq + bq).reshape(B, L, H, E)
        k = (keys @ Wk + bk).reshape(B, S, H, E)
        v = (values @ Wv + bv).reshape(B, S, H, E)
        scale = 1.0 / sqrt(E)
        scores = jnp.einsum('blhe,bshe->bhls', q, k)
        A = jax.nn.softmax(scale * scores, axis=-1)
        V = jnp.einsum('bhls,bshd->blhd', A, v)
        out = V.reshape(B, L, H * E) @ Wo + bo
        return out

    def _L0_ffn_ref(hidden_states, router_w, gate_w, up_w, down_w):
        import jax, jax.numpy as jnp
        import numpy as np
        S, B, H, I, E = (64, 2, 128, 352, 8)
        router_logits = jnp.einsum('sbh,eh->sbe', hidden_states, router_w)
        routing_indices = jnp.argmax(router_logits, axis=-1)
        out = jnp.zeros_like(hidden_states)
        for e in range(E):
            mask = (routing_indices == e)[..., None]
            xe = jnp.where(mask, hidden_states, 0.0)
            g = jnp.einsum('sbh,ih->sbi', xe, gate_w[e])
            u = jnp.einsum('sbh,ih->sbi', xe, up_w[e])
            ye = jnp.einsum('sbi,hi->sbh', jax.nn.silu(g) * u, down_w[e])
            out = out + jnp.where(mask, ye, 0.0)
        return out
    x = _layernorm(x + _L0_attn_ref(x, L0_attn_Wq, L0_attn_bq, L0_attn_Wk, L0_attn_bk, L0_attn_Wv, L0_attn_bv, L0_attn_Wo, L0_attn_bo), axis=-1)
    x = _layernorm(x + _L0_xattn_ref(x, ctx_1024, ctx_1024, L0_xattn_Wq, L0_xattn_bq, L0_xattn_Wk, L0_xattn_bk, L0_xattn_Wv, L0_xattn_bv, L0_xattn_Wo, L0_xattn_bo), axis=-1)
    x = _layernorm(x + _L0_ffn_ref(x, L0_ffn_router_w, L0_ffn_gate_w, L0_ffn_up_w, L0_ffn_down_w), axis=-1)
    return x

_drawn_inputs = setup_inputs


def setup_inputs(seed=0):
    import zlib

    import numpy as np

    out = dict(_drawn_inputs(seed))
    spreads = {'L0_attn_bq': (0.0, 0.1),
     'L0_attn_bk': (0.0, 0.8),
     'L0_attn_bv': (0.0, 0.1),
     'L0_attn_bo': (0.0, 0.1),
     'L0_xattn_bq': (0.0, 0.364),
     'L0_xattn_bk': (0.0, 0.8),
     'L0_xattn_bv': (0.0, 0.1),
     'L0_xattn_bo': (0.0, 0.1)}
    factors = {'L0_ffn_router_w': 6.194,
     'L0_ffn_gate_w': 5.883,
     'L0_ffn_up_w': 5.857,
     'L0_ffn_down_w': 5.84}
    for name, (base, spread) in spreads.items():
        noise = np.random.default_rng([zlib.crc32(name.encode()), seed]).standard_normal(out[name].shape)
        drawn = base * np.exp(spread * noise) if base else spread * noise
        out[name] = jnp.asarray(drawn.astype(out[name].dtype))
    for name, factor in factors.items():
        out[name] = (out[name] * factor).astype(out[name].dtype)
    return out
```

```python
from contextlib import ExitStack

import concourse.bass as bass
from concourse import mybir

F32 = mybir.dt.float32
F32R = mybir.dt.float32r
I32 = mybir.dt.int32
U32 = mybir.dt.uint32
ALU = mybir.AluOpType
ACT = mybir.ActivationFunctionType
AX = mybir.AxisListType

P = 128
LN_EPS = 1e-5
H, E = 16, 8
G, J = 4, 4
SCALE = 1.0 / float(E) ** 0.5
CEILING = 30.0
CH = 16

END = ("T0", "T1", "aT", "y2", "x2T", "lg")
PROJ = ("k2", "q2", "v2", "nq", "nk")
SELF = ("qk1", "v1", "s1", "p1T", "o1", "y1", "x1T")
SLOTS = {0: (("k2", "Y"),), 1: (("q2", "X"), ("T0", "X"), ("T1", "Y")), 2: (("qk1", "X"),), 3: (("v2", "Y"), ("aT", "X")),
         4: (("v1", "Y"),), 5: (("y2", "X"),), 6: (("s1", "Y"),), 7: (("nq", "X"),), 8: (("p1T", "Y"),), 9: (("nk", "X"),),
         10: (("o1", "Y"),), 11: (("x2T", "X"), ("y1", "Y")), 12: (("lg", "X"),), 14: (("x1T", "Y"),)}
ORDER = tuple(s for n in range(CH) for s in SLOTS.get(n, ()))
BANK = dict(ORDER)
LOOP = (2, 6)


def parts(i, B):
    return (END if 1 <= i <= B else ()) + (PROJ if 0 <= i + 1 < B else ()) + (SELF if 0 <= i + 2 < B else ())


def fill_numbers(B):
    at, count = {}, {"X": 0, "Y": 0}
    for i in range(-2, B + 1):
        for step, bank in ORDER:
            if step in parts(i, B):
                count[bank] += 1
                at[step, i] = count[bank]
    return at


def wait_apart(eng, w, sem, count):
    if isinstance(count, int):
        eng.wait_ge(sem, count)
        return
    eng.compute_val(count)
    eng.wait_ge(w["sem"], w["n"])
    eng.wait_ge(sem, count)


def attention(nc, ctx, w, io):
    B, S, D = io["x"].shape
    SC = io["ctxT"].shape[1] // B
    QT, KT = S // P, SC // P
    x_t = io["x"].rearrange("b (t p) d -> b p t d", p=P)
    at = fill_numbers(B)
    lo, hi = LOOP

    def number(step, i, back=0):
        if isinstance(i, int):
            return at[step, i - back]
        first = at[step, lo - back]
        each = at[step, lo + 1] - at[step, lo]
        return first + each * (i - lo)

    for step, _ in ORDER:
        for back in (0, 1):
            assert all(at[step, n - back] - at[step, lo - back] == (at[step, lo + 1] - at[step, lo]) * (n - lo)
                       for n in range(lo, hi))

    def x1T_of(b):
        return w["x1T"][:, bass.ds(b, 1)].rearrange("p b s -> p (b s)")

    def sb(name, shape, dt=F32):
        return ctx.enter_context(nc.sbuf_tensor(name, shape, dt))

    def sem(name):
        return ctx.enter_context(nc.semaphore(name))

    xTb = sb("xTb", [P, S])
    xrow = sb("xrow", [P, QT, D])
    xb = sb("xb", [P, QT, D])
    qkT1 = sb("qkT1", [P, 2, S])
    v1 = sb("v1", [P, QT, D])
    negmax1 = sb("negmax1", [P, QT])
    shift1 = sb("shift1", [P, QT])
    p1 = sb("p1", [P, QT, S])
    sum1 = sb("sum1", [P, QT])
    rsum1 = sb("rsum1", [P, QT])
    p1T = sb("p1T", [P, QT, S])
    o1T = sb("o1T", [P, S])
    t1 = sb("t1", [P, QT, D])
    st1 = sb("st1", [P, QT, 6])
    mv1 = sb("mv1", [P, QT, 2])
    ve1 = sb("ve1", [P, QT])
    rstd1 = sb("rstd1", [P, QT])
    x1 = sb("x1", [P, QT, D])
    ctxb = sb("ctxb", [P, SC])
    qsplit = sb("qsplit", [P, 2, S], F32R)
    ksplit = sb("ksplit", [P, 2, SC], F32R)
    sq = sb("sq", [P, S], F32R)
    sk = sb("sk", [P, SC], F32R)
    kst = sb("kst", [P, 2, G, SC], F32R)
    qrep = sb("qrep", [P, G, S])
    qst = sb("qst", [P, 2, G, J, S], F32R)
    vaug = sb("vaug", [P, 2, KT, H, 32])
    NP2 = 4
    p2 = sb("p2", [P, NP2, J * S])
    oS = sb("oS", [P, G, S])
    rden = sb("rden", [P, QT, H])
    att = sb("att", [P, QT, H, E])
    aT = sb("aT", [P, S])
    t2 = sb("t2", [P, QT, D])
    st2 = sb("st2", [P, QT, 6])
    mv2 = sb("mv2", [P, QT, 2])
    ve2 = sb("ve2", [P, QT])
    rstd2 = sb("rstd2", [P, QT])
    x2s = sb("x2s", [P, QT, D])
    x2T = sb("x2T", [P, S])
    half = sb("half", [P, QT])
    qd = nc.dram_tensor("q_parts", [2, P, S], F32).ap()
    kd = nc.dram_tensor("k_parts", [2, P, SC], F32).ap()

    psS = ctx.enter_context(nc.psum_tensor("psS", [P, 2, J * S], F32))
    psO = ctx.enter_context(nc.psum_tensor("psO", [P, G, S], F32))
    psX = ctx.enter_context(nc.psum_tensor("psX", [P, 512], F32))
    psY = ctx.enter_context(nc.psum_tensor("psY", [P, 512], F32))
    ps = {"X": psX, "Y": psY}

    filled = {"X": sem("X_filled"), "Y": sem("Y_filled")}
    taken = {"X": sem("X_taken"), "Y": sem("Y_taken")}
    xT_in, xrow_in, ctx_in = sem("xT_in"), sem("xrow_in"), sem("ctx_in")
    xb_ready, rstd1_ready, x1b_ready, rstd2_ready, x2_stored = (
        sem(n) for n in ("xb_ready", "rstd1_ready", "x1b_ready", "rstd2_ready", "x2_stored"))
    negmax_ready, shift_ready, rsum_ready = sem("negmax_ready"), sem("shift_ready"), sem("rsum_ready")
    t1_ready, st1_ready, mv1_ready, ve1_ready, x1_ready = (
        sem(n) for n in ("t1_ready", "st1_ready", "mv1_ready", "ve1_ready", "x1_ready"))
    t2_ready, st2_ready, mv2_ready, ve2_ready, x2_ready = (
        sem(n) for n in ("t2_ready", "st2_ready", "mv2_ready", "ve2_ready", "x2_ready"))
    qhigh_ready, khigh_ready, rden_ready = sem("qhigh_ready"), sem("khigh_ready"), sem("rden_ready")
    sq_ready, sk_ready = sem("sq_ready"), sem("sk_ready")
    heads_ready, vaug_cleared = sem("heads_ready"), sem("vaug_cleared")
    kd_in, qd_in, kst_in, qrep_in, qst_ready = (sem(n) for n in ("kd_in", "qd_in", "kst_in", "qrep_in", "qst_ready"))
    scores_done, probs_ready, pv_done, o_taken = (sem(n) for n in ("scores_done", "probs_ready", "pv_done", "o_taken"))

    block = ctx.enter_context(nc.Block())

    def rounds(eng, one):
        for i in range(-2, lo):
            one(i, i % 2, parts(i, B))
        with eng.Fori(0, (hi - lo) // 2) as r:
            for p in range(2):
                one(lo + p + 2 * r, p, parts(lo, B))
        for i in range(hi, B + 1):
            one(i, i % 2, parts(i, B))

    @block.sync
    def _(sp):
        for dst, src in w["loads"]:
            sp.dma_start(dst, src).then_inc(w["sem"], 16)

        def one(i, p, steps):
            later = not isinstance(i, int) or i > -2
            if "qk1" in steps:
                if later:
                    sp.wait_ge(filled["Y"], number("v1", i, 1))
                sp.dma_start(xTb[:], io["xT"][:, bass.ds((i + 2) * S, S)]).then_inc(xT_in, 16)
                if later:
                    sp.wait_ge(xb_ready, i + 2)
                sp.dma_start(xrow[:], x_t[bass.ds(i + 2, 1)].rearrange("b p t d -> p (b t) d")).then_inc(xrow_in, 16)
            if isinstance(i, int) and i == 0:
                sp.wait_ge(w["empty_ready"], 3)
                for dst, src in w["background"]:
                    sp.dma_start(dst, src).then_inc(w["background_in"], 16)
            if "k2" in steps:
                if not isinstance(i, int) or i > -1:
                    sp.wait_ge(filled["Y"], number("v2", i, 1))
                sp.dma_start(ctxb[:], io["ctxT"][:, bass.ds((i + 1) * SC, SC)]).then_inc(ctx_in, 16)
                q = 1 - p
                for n in (number("k2", i), number("q2", i), 64 * (i + 1), 16 * (i + 2), CH * i):
                    sp.compute_val(n)
                if not isinstance(i, int) or i >= 0:
                    sp.wait_ge(kst_in, 64 * (i + 1))
                    sp.wait_ge(qrep_in, 64 * (i + 1))
                sp.wait_ge(taken["Y"], number("k2", i))
                sp.dma_start(kd.rearrange("c p s -> p c s"), ksplit[:].bitcast(F32)).then_inc(kd_in, 16)
                sp.wait_ge(taken["X"], number("q2", i))
                sp.dma_start(qd.rearrange("c p s -> p c s"), qsplit[:].bitcast(F32)).then_inc(qd_in, 16)
                sp.wait_ge(kd_in, 16 * (i + 2))
                if not isinstance(i, int) or i >= 1:
                    sp.wait_ge(scores_done, CH * i)
                for c in range(4):
                    sp.dma_start(kst[32 * c:32 * c + 32, q].bitcast(F32),
                                 kd[c % 2].rearrange("(g r) s -> r g s", g=G)).then_inc(kst_in, 16)
                sp.wait_ge(qd_in, 16 * (i + 2))
                if not isinstance(i, int) or i >= 0:
                    sp.wait_ge(qst_ready, i + 1)
                for c in range(4):
                    sp.dma_start(qrep[32 * c:32 * c + 32],
                                 qd[c // 2].rearrange("(g r) s -> r g s", g=G)).then_inc(qrep_in, 16)
        rounds(sp, one)

    @block.tensor
    def _(pe):
        def mm(out_, l, r, start=True, stop=True, **k):
            return nc.tensor.matmul(out_, l, r, start=start, stop=stop, **k)

        def step(name, i, p):
            bank = ps[BANK[name]]
            fill = number(name, i)
            if not isinstance(fill, int) or fill > 1:
                pe.wait_ge(taken[BANK[name]], fill - 1)
            if name == "qk1":
                pe.wait_ge(xT_in, 16 * (i + 3))
                mm(bank[:, 0:S], w["wqk1"][:, 0], xTb[:])
                last = mm(bank[:, S:2 * S], w["wqk1"][:, 1], xTb[:])
            elif name == "v1":
                for n in range(QT):
                    last = mm(bank[:, n * D:(n + 1) * D], xTb[:, n * P:(n + 1) * P], w["wv1"][:])
            elif name == "s1":
                pe.wait_ge(taken["X"], number("qk1", i))
                for n in range(QT):
                    last = mm(bank[:, n * S:(n + 1) * S], qkT1[:, 0, n * P:(n + 1) * P], qkT1[:, 1, :])
            elif name == "p1T":
                for kt in range(QT):
                    for n in range(QT):
                        last = nc.tensor.transpose(bank[:, kt * S + n * P:kt * S + (n + 1) * P],
                                                   p1[:, n, kt * P:(kt + 1) * P], w["ident"])
            elif name == "o1":
                for kt in range(QT):
                    last = mm(bank[:, 0:S], v1[:, kt, :], p1T[:, kt, :], start=kt == 0, stop=kt == QT - 1)
            elif name == "y1":
                for n in range(QT):
                    last = mm(bank[:, n * D:(n + 1) * D], o1T[:, n * P:(n + 1) * P], w["wo1"][:])
            elif name == "x1T":
                pe.wait_ge(x1_ready, i + 3)
                for n in range(QT):
                    last = nc.tensor.transpose(bank[:, n * P:(n + 1) * P], x1[:, n, :], w["ident"])
            elif name == "q2":
                pe.wait_ge(taken["Y"], number("x1T", i, 1))
                last = mm(bank[:, 0:S], w["wq2"][:], x1T_of(i + 1))
            elif name == "k2":
                pe.wait_ge(ctx_in, 16 * (i + 2))
                last = mm(bank[:], w["wk2"][:], ctxb[:])
            elif name == "v2":
                for n in range(KT):
                    last = mm(bank[:, n * D:(n + 1) * D], ctxb[:, n * P:(n + 1) * P], w["wv2"][:])
            elif name == "nq":
                pe.wait_ge(sq_ready, i + 2)
                last = mm(bank[:, 0:S], w["heads"][:], sq[:])
            elif name == "nk":
                pe.wait_ge(sk_ready, i + 2)
                last = mm(bank[:], w["heads"][:], sk[:])
            elif name in ("T0", "T1"):
                n = int(name == "T1")
                pe.wait_ge(o_taken, 2 * i)
                for g in range(G):
                    last = nc.tensor.transpose(bank[:, g * P:(g + 1) * P], oS[:, g, n * P:(n + 1) * P], w["ident"])
            elif name == "aT":
                pe.wait_ge(taken["Y"], number("T1", i))
                for n in range(QT):
                    last = nc.tensor.transpose(bank[:, n * P:(n + 1) * P], att[:, n].rearrange("p h e -> p (h e)"), w["ident"])
            elif name == "y2":
                pe.wait_ge(taken["X"], number("aT", i))
                for n in range(QT):
                    last = mm(bank[:, n * D:(n + 1) * D], aT[:, n * P:(n + 1) * P], w["wo2"][:])
            elif name == "x2T":
                pe.wait_ge(x2_ready, i)
                for n in range(QT):
                    last = nc.tensor.transpose(bank[:, n * P:(n + 1) * P], x2s[:, n, :], w["ident"])
            else:
                pe.wait_ge(taken["X"], number("x2T", i))
                for n in range(QT):
                    last = mm(bank[:, 8 * n:8 * n + 8], x2T[:, n * P:(n + 1) * P], w["router"][:])
            last.then_inc(filled[BANK[name]], 1)

        def scores(i, p, c):
            g, kt = c // KT, c % KT
            if c == 0:
                pe.wait_ge(kst_in, 64 * (i + 1))
                pe.wait_ge(qst_ready, i + 1)
            if c >= 2 or not isinstance(i, int) or i > 0:
                pe.wait_ge(probs_ready, CH * i + c - 1)
            for jj in range(J // 2):
                last = mm(psS[:, c % 2, jj * 2 * S:(jj + 1) * 2 * S], kst[:, p, g, kt * P:(kt + 1) * P],
                          qst[:, p, g, 2 * jj:2 * jj + 2, :])
            last.then_inc(scores_done, 1)

        def times_v(i, p, c):
            g, kt = c // KT, c % KT
            if c % 8 == 0 and (not isinstance(i, int) or i > 0):
                pe.wait_ge(o_taken, 2 * i - 1 + c // 8)
            pe.wait_ge(probs_ready, CH * i + c + 1)
            for j in range(J):
                last = mm(psO[32 * j:32 * j + 32, g, :], vaug[:, p, kt, G * g + j, :], p2[:, c % NP2, j * S:(j + 1) * S],
                          start=kt == 0, stop=kt == KT - 1, tile_position=(0, 32 * j), skip_group_check=True)
            last.then_inc(pv_done, 1)

        def one(i, p, steps):
            cross = not isinstance(i, int) or 0 <= i < B
            for c in range(CH):
                if cross and c + 1 < CH:
                    scores(i, p, c + 1)
                if cross and c == CH - 1 and "k2" in steps:
                    scores(i + 1, 1 - p, 0)
                for name, _ in SLOTS.get(c, ()):
                    if name in steps:
                        step(name, i, p)
                if cross:
                    times_v(i, p, c)
            if isinstance(i, int) and i == -1:
                scores(0, 0, 0)

        pe.wait_ge(w["sem"], w["n"])
        pe.wait_ge(heads_ready, 1)
        pe.wait_ge(vaug_cleared, 2)
        rounds(pe, one)

    @block.scalar
    def _(act):
        def one(i, p, steps):
            cross = not isinstance(i, int) or 0 <= i < B
            for c in range(CH):
                if cross:
                    act.wait_ge(scores_done, CH * i + c + 1)
                    if c >= NP2 or not isinstance(i, int) or i > 0:
                        act.wait_ge(pv_done, CH * i + c + 1 - NP2)
                    nc.scalar.activation(p2[:, c % NP2, :], psS[:, c % 2, :], ACT.Exp, scale=SCALE,
                                         bias=-CEILING).then_inc(probs_ready, 1)
                if c == 3 and "qk1" in steps:
                    act.wait_ge(filled["X"], number("qk1", i))
                    nc.scalar.activation(qkT1[:, 0, :], psX[:, 0:S], ACT.Identity, bias=w["bcol"][:, 0:1])
                    nc.scalar.activation(qkT1[:, 1, :], psX[:, S:2 * S], ACT.Identity,
                                         bias=w["bcol"][:, 1:2]).then_inc(taken["X"], 1)
                if c == 7 and "s1" in steps:
                    act.wait_ge(shift_ready, i + 3)
                    for n in range(QT):
                        last = nc.scalar.activation(p1[:, n, :], psY[:, n * S:(n + 1) * S], ACT.Exp, scale=SCALE,
                                                    bias=shift1[:, n:n + 1], accum_out=sum1[:, n:n + 1])
                    last.then_inc(taken["Y"], 1)

        act.wait_ge(w["sem"], w["n"])
        rounds(act, one)

    @block.vector
    def _(dve):
        V = nc.vector

        def read(name, i):
            dve.wait_ge(filled[BANK[name]], number(name, i))
            return ps[BANK[name]]

        def took(name, ins):
            ins.then_inc(taken[BANK[name]], 1)

        def split(name, i, dst, n, bias, high_ready):
            bank = read(name, i)
            V.tensor_scalar(dst[:, 0, :], bank[:, 0:n], bias, None, ALU.add).then_inc(high_ready, 1)
            dve.wait_ge(high_ready, i + 2)
            took(name, V.scalar_tensor_tensor(dst[:, 1, :], bank[:, 0:n], bias, dst[:, 0, :].bitcast(F32),
                                              ALU.add, ALU.subtract))

        def statistics(src, src_ready, st, st_ready, mv, mv_ready, ve, ve_ready, count):
            dve.wait_ge(src_ready, count)
            for n in range(QT):
                last = V.bn_stats(st[:, n, :], src[:, n, :])
            last.then_inc(st_ready, 1)
            wait_apart(dve, w, st_ready, count)
            for n in range(QT):
                last = V.bn_aggr(mv[:, n, :], st[:, n, :])
            last.then_inc(mv_ready, 1)
            dve.wait_ge(mv_ready, count)
            V.tensor_scalar(ve[:], mv[:, :, 1], LN_EPS, None, ALU.add).then_inc(ve_ready, 1)

        def outputs(half, count):
            dve.wait_ge(pv_done, count)
            V.tensor_copy(oS[:, 2 * half:2 * half + 2], psO[:, 2 * half:2 * half + 2]).then_inc(o_taken, 1)

        def step(name, i, p):
            if name == "k2":
                if not isinstance(i, int) or i >= 0:
                    dve.wait_ge(kd_in, 16 * (i + 1))
                    dve.wait_ge(sk_ready, i + 1)
                split("k2", i, ksplit, SC, w["bcol"][:, 3:4], khigh_ready)
            elif name == "q2":
                if not isinstance(i, int) or i >= 0:
                    dve.wait_ge(qd_in, 16 * (i + 1))
                    dve.wait_ge(sq_ready, i + 1)
                split("q2", i, qsplit, S, w["bcol"][:, 2:3], qhigh_ready)
            elif name in ("T0", "T1"):
                n = int(name == "T1")
                T = read(name, i)[:].rearrange("p (h c) -> p h c", c=32)
                V.reciprocal(rden[:, n, :], T[:, :, E]).then_inc(rden_ready, 1)
                dve.wait_ge(rden_ready, 2 * i - 1 + n)
                took(name, V.tensor_tensor(att[:, n], T[:, :, 0:E], rden[:, n, :].unsqueeze(2).broadcast_to([P, H, E]), ALU.mult))
            elif name == "v2":
                if not isinstance(i, int) or i > 0:
                    dve.wait_ge(pv_done, CH * i)
                bank = read(name, i)
                took(name, V.tensor_tensor(vaug[:, 1 - p, :, :, 0:E], bank[:].rearrange("p (t h e) -> p t h e", t=KT, h=H),
                                           w["bv2"][:].rearrange("p (h e) -> p h e", h=H).unsqueeze(1).broadcast_to([P, KT, H, E]),
                                           ALU.add))
            elif name == "aT":
                took(name, V.tensor_copy(aT[:], read(name, i)[:, 0:S]))
            elif name == "v1":
                took(name, V.tensor_tensor(v1[:], read(name, i)[:, 0:QT * D].rearrange("p (t d) -> p t d", t=QT),
                                           w["bv1"][:].unsqueeze(1).broadcast_to([P, QT, D]), ALU.add))
            elif name == "y2":
                bank = read(name, i)
                dve.wait_ge(x1b_ready, i)
                V.tensor_tensor(t2[:], bank[:, 0:QT * D].rearrange("p (t d) -> p t d", t=QT), x1b_of(i - 1), ALU.add).then_inc(t2_ready, 1)
                dve.wait_ge(t2_ready, i)
                dve.sem_inc(taken[BANK[name]], 1)
                statistics(t2, t2_ready, st2, st2_ready, mv2, mv2_ready, ve2, ve2_ready, i)
            elif name == "s1":
                bank = read(name, i)
                V.tensor_reduce(negmax1[:], bank[:].rearrange("p (t k) -> p t k", t=QT), AX.X, ALU.max,
                                negate=True).then_inc(negmax_ready, 1)
                dve.wait_ge(negmax_ready, i + 3)
                V.tensor_scalar(shift1[:], negmax1[:], SCALE, None, ALU.mult).then_inc(shift_ready, 1)
            elif name == "nq":
                took(name, V.tensor_reduce(w["qnorm"][:, bass.ds(i + 1, 1)], read(name, i)[:, 0:S], AX.X, ALU.max))
            elif name == "nk":
                took(name, V.tensor_reduce(w["knorm"][:, bass.ds(i + 1, 1)], read(name, i)[:], AX.X, ALU.max))
            elif name == "p1T":
                bank = read(name, i)
                V.reciprocal(rsum1[:], sum1[:]).then_inc(rsum_ready, 1)
                took(name, V.tensor_copy(p1T[:].rearrange("p t d -> p (t d)"), bank[:]))
            elif name == "o1":
                took(name, V.tensor_copy(o1T[:], read(name, i)[:, 0:S]))
            elif name == "x2T":
                took(name, V.tensor_copy(x2T[:], read(name, i)[:, 0:S]))
            elif name == "y1":
                bank = read(name, i)
                dve.wait_ge(xb_ready, i + 3)
                dve.wait_ge(rsum_ready, i + 3)
                for n in range(QT):
                    last = V.scalar_tensor_tensor(t1[:, n, :], bank[:, n * D:(n + 1) * D], rsum1[:, n:n + 1], xb[:, n, :],
                                                  ALU.mult, ALU.add)
                last.then_inc(t1_ready, 1)
                dve.wait_ge(t1_ready, i + 3)
                dve.sem_inc(taken[BANK[name]], 1)
                statistics(t1, t1_ready, st1, st1_ready, mv1, mv1_ready, ve1, ve1_ready, i + 3)
            elif name == "lg":
                took(name, V.tensor_copy(w["logits"][:, bass.ds(QT * (i - 1), QT), :],
                                         read(name, i)[:, 0:8 * QT].rearrange("p (t e) -> p t e", t=QT)))
            elif name == "x1T":
                dve.wait_ge(rstd1_ready, i + 3)
                if not isinstance(i, int) or i > -2:
                    dve.wait_ge(x1b_ready, i + 2)
                for n in range(QT):
                    last = V.tensor_scalar(x1[:, n, :], t1[:, n, :], mv1[:, n, 0:1], rstd1[:, n:n + 1], ALU.subtract, ALU.mult)
                last.then_inc(x1_ready, 1)
                took(name, V.tensor_copy(x1T_of(i + 2), read(name, i)[:, 0:S]))

        def x1b_of(b):
            return w["x1b"][:, bass.ds(b, 1)].rearrange("p b t d -> p (b t) d")

        def one(i, p, steps):
            cross = not isinstance(i, int) or 0 <= i < B
            if not isinstance(i, int) or i >= 1:
                outputs(1, CH * i)
            for c in range(CH):
                for name, _ in SLOTS.get(c, ()):
                    if name in steps and name != "qk1":
                        step(name, i, p)
                if c == 6 and "y2" in steps:
                    dve.wait_ge(rstd2_ready, i)
                    if not isinstance(i, int) or i >= 2:
                        dve.wait_ge(x2_stored, i - 1)
                    for n in range(QT):
                        last = V.tensor_scalar(x2s[:, n, :], t2[:, n, :], mv2[:, n, 0:1], rstd2[:, n:n + 1], ALU.subtract, ALU.mult)
                    last.then_inc(x2_ready, 1)
                if c == 9 and cross:
                    outputs(0, CH * i + 8)

        dve.wait_ge(w["sem"], w["n"])
        V.tensor_copy(w["heads"][:], w["same_head"]).then_inc(heads_ready, 1)
        rounds(dve, one)

    @block.gpsimd
    def _(pool):
        Q = nc.gpsimd

        def one(i, p, steps):
            if "qk1" in steps:
                pool.wait_ge(xrow_in, 16 * (i + 3))
                if not isinstance(i, int) or i > -2:
                    pool.wait_ge(t1_ready, i + 2)
                Q.tensor_tensor(xb[:], xrow[:], w["bo1"][:].unsqueeze(1).broadcast_to([P, QT, D]), ALU.add).then_inc(xb_ready, 1)
            if "k2" in steps:
                if not isinstance(i, int) or i >= 0:
                    pool.wait_ge(filled["X"], number("nk", i, 1))
                pool.wait_ge(khigh_ready, i + 2)
                Q.tensor_tensor(sk[:], ksplit[:, 0, :].bitcast(F32), ksplit[:, 0, :].bitcast(F32), ALU.mult).then_inc(sk_ready, 1)
                pool.wait_ge(qhigh_ready, i + 2)
                Q.tensor_tensor(sq[:], qsplit[:, 0, :].bitcast(F32), qsplit[:, 0, :].bitcast(F32), ALU.mult).then_inc(sq_ready, 1)
            if "y2" in steps:
                pool.wait_ge(ve2_ready, i)
                Q.tensor_tensor(rstd2[:], ve2[:], half[:], ALU.pow).then_inc(rstd2_ready, 1)
            if "k2" in steps:
                pool.wait_ge(qrep_in, 64 * (i + 2))
                if not isinstance(i, int) or i >= 1:
                    wait_apart(pool, w, scores_done, CH * i)
                for j in range(J):
                    last = Q.tensor_scalar(qst[:, 1 - p, :, j, :], qrep[:], w["place"][:, j:j + 1], 1.0, ALU.mult, ALU.mult)
                last.then_inc(qst_ready, 1)
            if "y2" in steps:
                pool.wait_ge(x2_ready, i)
                Q.tensor_copy(w["x2"][:, bass.ds(QT * (i - 1), QT), 0:D], x2s[:]).then_inc(x2_stored, 1)
            if "qk1" in steps:
                pool.wait_ge(ve1_ready, i + 3)
                Q.tensor_tensor(rstd1[:], ve1[:], half[:], ALU.pow).then_inc(rstd1_ready, 1)
                pool.wait_ge(x1_ready, i + 3)
                Q.tensor_tensor(x1b_of(i + 2), x1[:], w["bo2"][:].unsqueeze(1).broadcast_to([P, QT, D]), ALU.add).then_inc(x1b_ready, 1)

        def x1b_of(b):
            return w["x1b"][:, bass.ds(b, 1)].rearrange("p b t d -> p (b t) d")

        Q.memset(vaug[:, :, :, :, E:32], 0.0).then_inc(vaug_cleared, 1)
        pool.wait_ge(vaug_cleared, 1)
        Q.memset(vaug[:, :, :, :, E:E + 1], 1.0).then_inc(vaug_cleared, 1)
        Q.memset(half[:], -0.5)
        Q.memset(w["empty"][:, 0:D], 0.0).then_inc(w["empty_ready"], 1)
        Q.memset(w["empty"][:, D:D + 4].bitcast(I32), B * S).then_inc(w["empty_ready"], 1)
        Q.iota(w["x2"][:, :, D:D + 4].bitcast(I32), [[P, B * QT], [0, 4]], base=0, channel_multiplier=1).then_inc(w["empty_ready"], 1)
        pool.wait_ge(w["sem"], w["n"])
        rounds(pool, one)
        pool.wait_ge(x2_stored, B)


def exact_attention(nc, ctx, w, io):
    B, S, D = io["x"].shape
    SC = io["ctxT"].shape[1] // B
    QT, KT = S // P, SC // P
    CHUNKS, MAXIMA = G * KT, H * QT

    def sb(name, shape, dt=F32):
        return ctx.enter_context(nc.sbuf_tensor(name, shape, dt))

    def sem(name):
        return ctx.enter_context(nc.semaphore("e_" + name))

    prod = sb("norm_products", [P, B])
    worst = sb("worst", [P, 1])
    worst_all = sb("worst_all", [1, 1])
    unbounded = sb("unbounded", [1, 1], I32)
    ctxb = sb("e_ctxb", [P, SC])
    qsplit = sb("e_qsplit", [P, 2, S], F32R)
    ksplit = sb("e_ksplit", [P, 2, SC], F32R)
    kst = sb("e_kst", [P, G, SC], F32R)
    qst = sb("e_qst", [P, G, J, S], F32R)
    vaug = sb("e_vaug", [P, KT, H, 32])
    m2 = sb("e_maxima", [P, QT, J, G])
    msplit = sb("e_msplit", [H, 2, S], F32R)
    p2 = sb("e_p2", [P, 2, J * S])
    oS = sb("e_oS", [P, G, S])
    rden = sb("e_rden", [P, QT, H])
    att = sb("e_att", [P, QT, H, E])
    aT = sb("e_aT", [P, S])
    t2 = sb("e_t2", [P, QT, D])
    st2 = sb("e_st2", [P, QT, 6])
    mv2 = sb("e_mv2", [P, QT, 2])
    ve2 = sb("e_ve2", [P, QT])
    rstd2 = sb("e_rstd2", [P, QT])
    x2s = sb("e_x2s", [P, QT, D])
    x2T = sb("e_x2T", [P, S])
    half = sb("e_half", [P, QT])
    qd = nc.dram_tensor("e_q_parts", [2, P, S], F32).ap()
    kd = nc.dram_tensor("e_k_parts", [2, P, SC], F32).ap()
    md = nc.dram_tensor("e_m_parts", [H, 2, S], F32).ap()
    psS = ctx.enter_context(nc.psum_tensor("e_psS", [P, 2, J * S], F32))
    psO = ctx.enter_context(nc.psum_tensor("e_psO", [P, G, S], F32))
    psX = ctx.enter_context(nc.psum_tensor("e_psX", [P, 512], F32))
    psY = ctx.enter_context(nc.psum_tensor("e_psY", [P, 512], F32))

    worst_ready, worst_turned, decided = sem("worst_ready"), sem("worst_turned"), sem("decided")
    cleared, vaug_cleared, start = sem("cleared"), sem("vaug_cleared"), sem("batch_may_start")
    names = ("q2", "k2", "v2", "mT", "T0", "T1", "aT", "y2", "x2T", "lg")
    done = {n: sem(n + "_done") for n in names}
    took = {n: sem(n + "_taken") for n in names}
    ctx_in, kd_in, qd_in, md_in = sem("ctx_in"), sem("k_parts_out"), sem("q_parts_out"), sem("m_parts_out")
    kst_in, qst_in, mst_in = sem("kst_in"), sem("qst_in"), sem("m_rows_in")
    max_done, max_taken, scores_done, probs_ready, pv_done = (
        sem(n) for n in ("max_scores_done", "maximum_taken", "scores_done", "probs_ready", "pv_done"))
    o_taken, ve2_ready, rstd2_ready, x2_ready, step_done = (
        sem(n) for n in ("o_taken", "ve2_ready", "rstd2_ready", "x2_ready", "dve_step_done"))
    CLEARED = 5

    def for_batches(eng, one):
        eng.wait_ge(decided, 1)
        flag = eng.value_load(unbounded[0:1, 0:1], min_val=0, max_val=1)
        with eng.If(flag > 0):
            with eng.Fori(0, B) as b:
                eng.wait_ge(start, b + CLEARED)
                one(b)

    block = ctx.enter_context(nc.Block())

    @block.sync
    def _(sp):
        def one(b):
            sp.dma_start(ctxb[:], io["ctxT"][:, bass.ds(b * SC, SC)]).then_inc(ctx_in, 16)
            sp.wait_ge(took["k2"], b + 1)
            sp.dma_start(kd.rearrange("c p s -> p c s"), ksplit[:].bitcast(F32)).then_inc(kd_in, 16)
            sp.wait_ge(took["q2"], b + 1)
            sp.dma_start(qd.rearrange("c p s -> p c s"), qsplit[:].bitcast(F32)).then_inc(qd_in, 16)
            sp.wait_ge(kd_in, 16 * (b + 1))
            for c, part in enumerate((0, 1, 0)):
                sp.dma_start(kst[32 * c:32 * c + 32].bitcast(F32), kd[part].rearrange("(g r) s -> r g s", g=G)).then_inc(kst_in, 16)
            sp.wait_ge(qd_in, 16 * (b + 1))
            for c, part in enumerate((0, 0, 1)):
                for j in range(J):
                    r = 32 * c + E * j
                    sp.dma_start(qst[r:r + E, :, j, :].bitcast(F32),
                                 qd[part].rearrange("(g r) s -> r g s", g=G)[E * j:E * j + E]).then_inc(qst_in, 16)
            sp.wait_ge(took["mT"], b + 1)
            sp.dma_start(md, msplit[:].bitcast(F32)).then_inc(md_in, 16)
            sp.wait_ge(md_in, 16 * (b + 1))
            for j in range(J):
                r = 96 + E * j
                sp.dma_start(qst[r:r + 2, :, j, :].bitcast(F32),
                             md[G * j:G * j + G].rearrange("g r s -> r g s")).then_inc(mst_in, 16)

        for_batches(sp, one)

    @block.tensor
    def _(pe):
        def mm(out_, l, r, start_=True, stop=True, **k):
            return nc.tensor.matmul(out_, l, r, start=start_, stop=stop, **k)

        pe.wait_ge(worst_ready, 1)
        nc.tensor.transpose(psX[0:1, 0:P], worst[:], w["ident"]).then_inc(worst_turned, 1)

        def one(b):
            x1T_b = w["x1T"][:, bass.ds(b, 1)].rearrange("p b s -> p (b s)")
            pe.wait_ge(ctx_in, 16 * (b + 1))
            mm(psY[:], w["wk2"][:], ctxb[:]).then_inc(done["k2"], 1)
            mm(psX[:, 0:S], w["wq2"][:], x1T_b).then_inc(done["q2"], 1)
            pe.wait_ge(took["q2"], b + 1)
            for t in range(KT):
                last = mm(psX[:, t * D:(t + 1) * D], ctxb[:, t * P:(t + 1) * P], w["wv2"][:])
            last.then_inc(done["v2"], 1)
            pe.wait_ge(took["k2"], b + 1)
            pe.wait_ge(took["v2"], b + 1)
            pe.wait_ge(kst_in, 48 * (b + 1))
            pe.wait_ge(qst_in, 192 * (b + 1))
            for n in range(MAXIMA):
                g, j, t = n // (J * QT), n // QT % J, n % QT
                if n >= 2:
                    pe.wait_ge(max_taken, MAXIMA * b + n - 1)
                mm((psY, psX)[n % 2][:], qst[0:96, g, j, t * P:(t + 1) * P], kst[0:96, g, :]).then_inc(max_done, 1)
            pe.wait_ge(max_taken, MAXIMA * (b + 1))
            for t in range(QT):
                last = nc.tensor.transpose(psY[0:H, t * P:(t + 1) * P], m2[:, t].rearrange("p j g -> p (j g)"), w["ident"])
            last.then_inc(done["mT"], 1)
            pe.wait_ge(mst_in, 64 * (b + 1))
            for c in range(CHUNKS):
                g, kt = c // KT, c % KT
                if c >= 2:
                    pe.wait_ge(probs_ready, CHUNKS * b + c - 1)
                for jj in range(J // 2):
                    last = mm(psS[:, c % 2, jj * 2 * S:(jj + 1) * 2 * S], kst[:, g, kt * P:(kt + 1) * P], qst[:, g, 2 * jj:2 * jj + 2, :])
                last.then_inc(scores_done, 1)
                pe.wait_ge(probs_ready, CHUNKS * b + c + 1)
                for j in range(J):
                    last = mm(psO[32 * j:32 * j + 32, g, :], vaug[:, kt, G * g + j, :], p2[:, c % 2, j * S:(j + 1) * S],
                              start_=kt == 0, stop=kt == KT - 1, tile_position=(0, 32 * j), skip_group_check=True)
                last.then_inc(pv_done, 1)
            pe.wait_ge(o_taken, b + 1)
            for n, (name, bank) in enumerate((("T0", psX), ("T1", psY))):
                for g in range(G):
                    last = nc.tensor.transpose(bank[:, g * P:(g + 1) * P], oS[:, g, n * P:(n + 1) * P], w["ident"])
                last.then_inc(done[name], 1)
            pe.wait_ge(took["T1"], b + 1)
            for n in range(QT):
                last = nc.tensor.transpose(psX[:, n * P:(n + 1) * P], att[:, n].rearrange("p h e -> p (h e)"), w["ident"])
            last.then_inc(done["aT"], 1)
            pe.wait_ge(took["aT"], b + 1)
            for n in range(QT):
                last = mm(psY[:, n * D:(n + 1) * D], aT[:, n * P:(n + 1) * P], w["wo2"][:])
            last.then_inc(done["y2"], 1)
            pe.wait_ge(x2_ready, b + 1)
            for n in range(QT):
                last = nc.tensor.transpose(psX[:, n * P:(n + 1) * P], x2s[:, n, :], w["ident"])
            last.then_inc(done["x2T"], 1)
            pe.wait_ge(took["x2T"], b + 1)
            for n in range(QT):
                last = mm(psY[:, 8 * n:8 * n + 8], x2T[:, n * P:(n + 1) * P], w["router"][:])
            last.then_inc(done["lg"], 1)

        for_batches(pe, one)

    @block.scalar
    def _(act):
        def one(b):
            for c in range(CHUNKS):
                if c >= 2:
                    act.wait_ge(pv_done, CHUNKS * b + c - 1)
                act.wait_ge(scores_done, CHUNKS * b + c + 1)
                nc.scalar.activation(p2[:, c % 2, :], psS[:, c % 2, :], ACT.Exp, scale=SCALE).then_inc(probs_ready, 1)

        for_batches(act, one)

    @block.vector
    def _(dve):
        V = nc.vector
        V.tensor_tensor(prod[:], w["qnorm"][:], w["knorm"][:], ALU.mult).then_inc(step_done, 1)
        dve.wait_ge(step_done, 1)
        V.tensor_reduce(worst[:], prod[:], AX.X, ALU.max).then_inc(worst_ready, 1)
        V.memset(kst[96:128].rearrange("p g s -> p (g s)").bitcast(F32), 1.0).then_inc(start, 1)
        V.memset(qst[:].rearrange("p g j s -> p (g j s)").bitcast(F32), 0.0).then_inc(start, 1)
        dve.wait_ge(worst_turned, 1)
        V.tensor_reduce(worst_all[:], psX[0:1, 0:P], AX.X, ALU.max).then_inc(step_done, 1)
        dve.wait_ge(step_done, 2)
        V.tensor_scalar(unbounded[:], worst_all[:], 0.98 * (CEILING / SCALE) ** 2, 0.0, ALU.is_le, ALU.is_equal).then_inc(decided, 1)
        LINKS = 10

        def one(b):
            links = [0]

            def link(ins):
                links[0] += 1
                ins.then_inc(step_done, 1)
                wait_apart(dve, w, step_done, LINKS * b + links[0] + 2)

            def read(name, bank):
                dve.wait_ge(done[name], b + 1)
                return bank

            def split(name, dst, bank, n, bias):
                read(name, bank)
                link(V.tensor_scalar(dst[:, 0, :], bank[:, 0:n], bias, None, ALU.add))
                V.scalar_tensor_tensor(dst[:, 1, :], bank[:, 0:n], bias, dst[:, 0, :].bitcast(F32),
                                       ALU.add, ALU.subtract).then_inc(took[name], 1)

            split("k2", ksplit, psY, SC, w["bcol"][:, 3:4])
            split("q2", qsplit, psX, S, w["bcol"][:, 2:3])
            V.tensor_tensor(vaug[:, :, :, 0:E], read("v2", psX)[:].rearrange("p (t h e) -> p t h e", t=KT, h=H),
                            w["bv2"][:].rearrange("p (h e) -> p h e", h=H).unsqueeze(1).broadcast_to([P, KT, H, E]),
                            ALU.add).then_inc(took["v2"], 1)
            for n in range(MAXIMA):
                g, j, t = n // (J * QT), n // QT % J, n % QT
                dve.wait_ge(max_done, MAXIMA * b + n + 1)
                V.tensor_reduce(m2[:, t, j, g:g + 1], (psY, psX)[n % 2][:], AX.X, ALU.max).then_inc(max_taken, 1)
            read("mT", psY)
            link(V.tensor_scalar(msplit[:, 0, :], psY[0:H, 0:S], -1.0, None, ALU.mult))
            V.scalar_tensor_tensor(msplit[:, 1, :], psY[0:H, 0:S], -1.0, msplit[:, 0, :].bitcast(F32),
                                   ALU.mult, ALU.subtract).then_inc(took["mT"], 1)
            dve.wait_ge(pv_done, CHUNKS * (b + 1))
            V.tensor_copy(oS[:], psO[:]).then_inc(o_taken, 1)
            for n, (name, bank) in enumerate((("T0", psX), ("T1", psY))):
                T = read(name, bank)[:].rearrange("p (h c) -> p h c", c=32)
                link(V.reciprocal(rden[:, n, :], T[:, :, E]))
                V.tensor_tensor(att[:, n], T[:, :, 0:E], rden[:, n, :].unsqueeze(2).broadcast_to([P, H, E]),
                                ALU.mult).then_inc(took[name], 1)
            V.tensor_copy(aT[:], read("aT", psX)[:, 0:S]).then_inc(took["aT"], 1)
            link(V.tensor_tensor(t2[:], read("y2", psY)[:, 0:QT * D].rearrange("p (t d) -> p t d", t=QT),
                                 w["x1b"][:, bass.ds(b, 1)].rearrange("p b t d -> p (b t) d"), ALU.add))
            for n in range(QT):
                last = V.bn_stats(st2[:, n, :], t2[:, n, :])
            link(last)
            for n in range(QT):
                last = V.bn_aggr(mv2[:, n, :], st2[:, n, :])
            link(last)
            V.tensor_scalar(ve2[:], mv2[:, :, 1], LN_EPS, None, ALU.add).then_inc(ve2_ready, 1)
            dve.wait_ge(rstd2_ready, b + 1)
            for n in range(QT):
                last = V.tensor_scalar(x2s[:, n, :], t2[:, n, :], mv2[:, n, 0:1], rstd2[:, n:n + 1], ALU.subtract, ALU.mult)
            last.then_inc(x2_ready, 1)
            dve.wait_ge(x2_ready, b + 1)
            link(V.tensor_copy(w["x2"][:, bass.ds(QT * b, QT), 0:D], x2s[:]))
            V.tensor_copy(x2T[:], read("x2T", psX)[:, 0:S]).then_inc(took["x2T"], 1)
            link(V.tensor_copy(w["logits"][:, bass.ds(QT * b, QT), :],
                               read("lg", psY)[:, 0:8 * QT].rearrange("p (t e) -> p t e", t=QT)))
            assert links[0] == LINKS
            dve.sem_inc(start, 1)

        for_batches(dve, one)

    @block.gpsimd
    def _(pool):
        Q = nc.gpsimd
        Q.memset(vaug[:, :, :, E:32], 0.0).then_inc(vaug_cleared, 1)
        pool.wait_ge(vaug_cleared, 1)
        Q.memset(vaug[:, :, :, E:E + 1], 1.0).then_inc(start, 1)
        Q.memset(half[:], -0.5).then_inc(start, 2)

        def one(b):
            pool.wait_ge(ve2_ready, b + 1)
            Q.tensor_tensor(rstd2[:], ve2[:], half[:], ALU.pow).then_inc(rstd2_ready, 1)

        for_batches(pool, one)


def experts(nc, ctx, w, io):
    out = io["out"].rearrange("b s d -> (b s) d")
    NTOK, D = out.shape
    NT, NE, F = NTOK // P, w["logits"].shape[2], w["gu"].shape[2] // 2
    NS = w["slots"].shape[0] // P
    FC = w["down"].shape[2]
    tail = F - (FC - 1) * P

    def sb(name, shape, dt=F32):
        return ctx.enter_context(nc.sbuf_tensor(name, shape, dt))

    def sem(name):
        return ctx.enter_context(nc.semaphore(name))

    top = sb("top", [P, NT])
    is_top = sb("is_top", [P, NT, NE])
    rank = sb("rank", [P, NT, NE])
    first = sb("first", [P, NT])
    chosen = sb("chosen", [P, NT, NE])
    total = sb("total", [P, NE, NT])
    upto = sb("upto", [P, NE, NT])
    before = sb("before", [P, NE, NT])
    over = sb("over", [P, NE, NT])
    tiles = sb("tiles", [P, NE])
    ends = sb("ends", [P, NE])
    base = sb("base", [P, NE])
    local = sb("local", [P, NT, NE])
    place = sb("slot_all", [P, NT, NE])
    mine = sb("slot_mine", [P, NT, NE])
    slot_f = sb("slot_f", [P, NT])
    slot = sb("slot", [P, NT], U32)
    past = sb("past", [P, NS, NE])
    expert_f = sb("expert_f", [P, NS])
    expert = sb("expert", [P, NS], I32)
    LEAD = 6
    xs = sb("xs", [P, NS, D + 4])
    x_turn = sb("x_turn", [P, 2, D])
    token = sb("token", [P, 2], U32)
    xsT = sb("xsT", [P, 2, P])
    silu = sb("silu", [P, 2, F])
    hid = sb("hid", [P, 2, FC * P])
    hidT = sb("hidT", [P, 2, FC, P])
    t3 = sb("t3", [P, 2, D])
    st3 = sb("st3", [P, 2, 6])
    mv3 = sb("mv3", [P, 2, 2])
    ve3 = sb("ve3", [P, 2])
    rstd3 = sb("rstd3", [P, 2])
    y3 = sb("y3", [P, 2, D])
    half3 = sb("half3", [P, 1])
    psX = ctx.enter_context(nc.psum_tensor("psXs", [P, 512], F32))
    psG = ctx.enter_context(nc.psum_tensor("psG", [P, 2, 512], F32))
    psU = ctx.enter_context(nc.psum_tensor("psU", [P, 2, 512], F32))
    psH = ctx.enter_context(nc.psum_tensor("psH", [P, 512], F32))
    psY = ctx.enter_context(nc.psum_tensor("psYs", [P, 2, 512], F32))

    routed, chosen_ready, counted = sem("routed"), sem("chosen_ready"), sem("counted")
    slot_ready, expert_ready, scattered = sem("slot_ready"), sem("expert_ready"), sem("scattered")
    xs_in, token_ready = sem("tiles_in"), sem("token_ready")
    x_turn_in = [sem("even_tile_in"), sem("odd_tile_in")]
    stored = [sem("even_rows_stored"), sem("odd_rows_stored")]
    xT_done, xT_taken, gu_done, silu_ready = (sem(n) for n in ("xs_turned", "xsT_ready", "gu_done", "silu_ready"))
    hid_ready, hT_done, hT_taken, y_done, t3_ready = (sem(n) for n in ("hid_ready", "hid_turned", "hidT_ready", "y_done", "t3_ready"))
    st3_ready, mv3_ready, ve3_ready, rstd3_ready, y3_ready = (
        sem(n) for n in ("st3_ready", "mv3_ready", "ve3_ready", "rstd3_ready", "y3_ready"))
    hid_cleared, half_set = sem("hid_cleared"), sem("half_set")
    c = w["route_consts"]
    block = ctx.enter_context(nc.Block())
    tile_rows = w["slots"].rearrange("(s p) c -> p s c", p=P)

    def pipeline(eng, one):
        loops = (NS - 1 - LEAD) // 2
        for s in range(LEAD):
            one(s, s % 2, s // 2)
        with eng.Fori(0, loops) as r:
            for p in range(2):
                one(LEAD + p + 2 * r, p, LEAD // 2 + r)
        for s in range(LEAD + 2 * loops, NS + 3):
            one(s, s % 2, s // 2)

    def inside(s, back):
        return not isinstance(s, int) or 0 <= s - back < NS

    def of(tiles, s):
        return tiles[:, bass.ds(s, 1)].rearrange("p s c -> p (s c)")

    @block.vector
    def _(dve):
        V = nc.vector
        steps = [0]

        def link(ins):
            steps[0] += 1
            ins.then_inc(routed, 1)
            dve.wait_ge(routed, steps[0])

        def by_expert(a):
            return a.unsqueeze(1).broadcast_to([P, NT, NE])

        V.memset(hid[:], 0.0).then_inc(hid_cleared, 1)
        link(V.tensor_reduce(top[:], w["logits"][:], AX.X, ALU.max))
        link(V.tensor_tensor(is_top[:], w["logits"][:], top[:].unsqueeze(2).broadcast_to([P, NT, NE]), ALU.is_equal))
        link(V.tensor_tensor(rank[:], is_top[:], by_expert(c["rank"]), ALU.mult))
        link(V.tensor_reduce(first[:], rank[:], AX.X, ALU.max))
        V.tensor_tensor(chosen[:], rank[:], first[:].unsqueeze(2).broadcast_to([P, NT, NE]), ALU.is_equal).then_inc(chosen_ready, 1)
        dve.wait_ge(counted, 1)
        link(V.tensor_copy(total[:], psU[:, 0, 0:NT * NE].rearrange("p (t e) -> p e t", t=NT)))
        flat = lambda a: a.rearrange("p e t -> p (e t)")
        link(V.tensor_tensor_scan(flat(upto[:]), c["within"], flat(total[:]), 0.0, ALU.mult, ALU.add))
        link(V.tensor_tensor(before[:], upto[:], total[:], ALU.subtract))
        link(V.tensor_tensor(over[:], upto[:, :, NT - 1:NT].broadcast_to([P, NE, NT]),
                             c["steps"].unsqueeze(1).broadcast_to([P, NE, NT]), ALU.is_gt))
        link(V.tensor_reduce(tiles[:], over[:], AX.X, ALU.add))
        link(V.tensor_tensor_scan(ends[:], c["ones8"], tiles[:], 0.0, ALU.mult, ALU.add))
        link(V.tensor_tensor(base[:], ends[:], tiles[:], ALU.subtract))
        link(V.tensor_tensor(local[:], psG[:, 0, 0:NT * NE].rearrange("p (t e) -> p t e", t=NT),
                             before[:].rearrange("p e t -> p t e"), ALU.add))
        link(V.scalar_tensor_tensor(place[:], by_expert(base[:]), float(P), local[:], ALU.mult, ALU.add))
        link(V.tensor_tensor(mine[:], place[:], chosen[:], ALU.mult))
        link(V.tensor_reduce(slot_f[:], mine[:], AX.X, ALU.add))
        V.tensor_copy(slot[:], slot_f[:]).then_inc(slot_ready, 1)
        link(V.tensor_tensor(past[:], ends[:].unsqueeze(1).broadcast_to([P, NS, NE]),
                             c["tile"].unsqueeze(2).broadcast_to([P, NS, NE]), ALU.is_le))
        link(V.tensor_reduce(expert_f[:], past[:], AX.X, ALU.add))
        V.tensor_scalar(expert[:], expert_f[:], float(NE - 1), None, ALU.min).then_inc(expert_ready, 1)

        def one(s, p, h):
            if inside(s, 0):
                dve.wait_ge(silu_ready, s + 1)
                if inside(s, 2):
                    dve.wait_ge(hT_done, s - 1)
                V.tensor_tensor(hid[:, p, 0:F], silu[:, p, :], psU[:, p, 0:F], ALU.mult).then_inc(hid_ready, 1)
            if inside(s, 3):
                dve.wait_ge(rstd3_ready, s - 2)
                if inside(s, 5):
                    dve.wait_ge(stored[1 - p], 16 * (h - 2 + p))
                V.tensor_scalar(y3[:, 1 - p], t3[:, 1 - p], mv3[:, 1 - p, 0:1], rstd3[:, 1 - p:2 - p],
                                ALU.subtract, ALU.mult).then_inc(y3_ready, 1)
            if inside(s, 2):
                dve.wait_ge(y_done, s - 1)
                if isinstance(s, int) and s == 2:
                    dve.wait_ge(xs_in, 16)
                V.tensor_tensor(t3[:, p], psY[:, p, 0:D], of(xs, s - 2)[:, 0:D], ALU.add).then_inc(t3_ready, 1)
                dve.wait_ge(t3_ready, s - 1)
                V.bn_stats(st3[:, p], t3[:, p]).then_inc(st3_ready, 1)
                wait_apart(dve, w, st3_ready, s - 1)
                V.bn_aggr(mv3[:, p], st3[:, p]).then_inc(mv3_ready, 1)
                dve.wait_ge(mv3_ready, s - 1)
                V.tensor_scalar(ve3[:, p:p + 1], mv3[:, p, 1:2], LN_EPS, None, ALU.add).then_inc(ve3_ready, 1)

        pipeline(dve, one)

    @block.tensor
    def _(pe):
        def mm(out_, l, r, start=True, stop=True):
            return nc.tensor.matmul(out_, l, r, start=start, stop=stop)

        pe.wait_ge(chosen_ready, 1)
        one_hot = chosen[:].rearrange("p t e -> p (t e)")
        mm(psG[:, 0, 0:NT * NE], c["earlier"], one_hot)
        mm(psU[:, 0, 0:NT * NE], c["ones"], one_hot).then_inc(counted, 1)
        pe.wait_ge(expert_ready, 1)
        pe.wait_ge(w["background_in"], 16 * len(w["background"]))

        def turn(p, h):
            pe.wait_ge(x_turn_in[p], 16 * (h + 1))
            nc.tensor.transpose(psX[:, 0:P], x_turn[:, p, :], w["ident"]).then_inc(xT_done, 1)

        def one(s, p, h):
            if inside(s, 0):
                e = pe.value_load(expert[0:1, bass.ds(s, 1)], min_val=0, max_val=NE - 1)
                pe.wait_ge(xT_taken, s + 1)
                if inside(s, 2):
                    pe.wait_ge(hid_ready, s - 1)
                for n, bank in ((0, psG), (1, psU)):
                    last = mm(bank[:, p, 0:F], xsT[:, p, :], w["gu"][:, bass.ds(e, 1), n * F:(n + 1) * F].rearrange("k e n -> k (e n)"))
                last.then_inc(gu_done, 1)
            if inside(s, -1):
                turn(1 - p, h + p)
            if inside(s, 2):
                e = pe.value_load(expert[0:1, bass.ds(s - 2, 1)], min_val=0, max_val=NE - 1)
                pe.wait_ge(hT_taken, s - 1)
                if inside(s, 4):
                    pe.wait_ge(t3_ready, s - 3)
                for n in range(FC):
                    k = P if n < FC - 1 else tail
                    last = mm(psY[:, p, 0:D], hidT[0:k, p, n, :], w["down"][0:k, bass.ds(e, 1), n, :].rearrange("k e n -> k (e n)"),
                              start=n == 0, stop=n == FC - 1)
                last.then_inc(y_done, 1)
            if inside(s, 1):
                pe.wait_ge(hid_ready, s)
                if inside(s, 2):
                    pe.wait_ge(hT_taken, s - 1)
                for n in range(FC):
                    last = nc.tensor.transpose(psH[:, n * P:(n + 1) * P], hid[:, 1 - p, n * P:(n + 1) * P], w["ident"])
                last.then_inc(hT_done, 1)

        pe.wait_ge(hid_cleared, 1)
        turn(0, 0)
        pipeline(pe, one)

    @block.scalar
    def _(act):
        def turned(s, p):
            act.wait_ge(xT_done, s + 1)
            if inside(s, 2):
                act.wait_ge(gu_done, s - 1)
            nc.scalar.activation(xsT[:, p, :], psX[:, 0:P], ACT.Identity).then_inc(xT_taken, 1)

        def one(s, p, h):
            if inside(s, 0):
                act.wait_ge(gu_done, s + 1)
                if inside(s, 2):
                    act.wait_ge(hid_ready, s - 1)
                nc.scalar.activation(silu[:, p, :], psG[:, p, 0:F], ACT.Silu).then_inc(silu_ready, 1)
            if inside(s, -1):
                turned(s + 1, 1 - p)
            if inside(s, 1):
                act.wait_ge(hT_done, s)
                if inside(s, 3):
                    act.wait_ge(y_done, s - 2)
                nc.scalar.activation(hidT[:, 1 - p].rearrange("p n t -> p (n t)"), psH[:, 0:FC * P], ACT.Identity).then_inc(hT_taken, 1)

        turned(0, 0)
        pipeline(act, one)

    @block.sync
    def _(sp):
        sp.wait_ge(scattered, 16 * NT)

        def one(s, p, h):
            if inside(s, 0):
                if inside(s, 2):
                    sp.wait_ge(xT_done, s - 1)
                sp.dma_start(x_turn[:, p], of(tile_rows, s)[:, 0:D]).then_inc(x_turn_in[p], 16)
            if isinstance(s, int) and s == 1:
                sp.dma_start(xs[:], tile_rows).then_inc(xs_in, 16)

        pipeline(sp, one)

    @block.gpsimd
    def _(pool):
        nc.gpsimd.memset(half3[:], -0.5).then_inc(half_set, 1)
        pool.wait_ge(half_set, 1)
        pool.wait_ge(slot_ready, 1)
        pool.wait_ge(w["background_in"], 16 * len(w["background"]))
        for t in range(NT):
            nc.gpsimd.indirect_dma_start(out=w["slots"], out_offset=bass.IndirectOffsetOnAxis(ap=slot[:, t:t + 1], axis=0),
                                         in_=w["x2"][:, t, :], in_offset=None).then_inc(scattered, 16)

        def one(s, p, h):
            if inside(s, 2):
                pool.wait_ge(ve3_ready, s - 1)
                nc.gpsimd.tensor_tensor(rstd3[:, p:p + 1], ve3[:, p:p + 1], half3[:], ALU.pow).then_inc(rstd3_ready, 1)
            if inside(s, 3):
                Q = nc.gpsimd
                if inside(s, 5):
                    pool.wait_ge(stored[1 - p], 16 * (h - 2 + p))
                Q.tensor_copy(token[:, 1 - p:2 - p], of(xs, s - 3)[:, D:D + 1].bitcast(U32)).then_inc(token_ready, 1)
                wait_apart(pool, w, token_ready, s - 2)
                pool.wait_ge(y3_ready, s - 2)
                Q.indirect_dma_start(out=out, out_offset=bass.IndirectOffsetOnAxis(ap=token[:, 1 - p:2 - p], axis=0),
                                     in_=y3[:, 1 - p, :], in_offset=None, bounds_check=NTOK - 1,
                                     oob_is_err=False).then_inc(stored[1 - p], 16)

        pipeline(pool, one)
        for p in range(2):
            pool.wait_ge(stored[p], 16 * ((NS + 1 - p) // 2))


def decoder_layer(nc, x, xT, ctxT, Wq1, bq1, Wk1, bk1, Wv1, bv1, Wo1, bo1, Wq2, bq2, Wk2, bk2, Wv2, bv2, Wo2, bo2,
                  routerT, gate_up, down, shape_consts, out):
    B, S, D = x.shape
    NT = B * S // P
    NE, F = down.shape[0], down.shape[1]
    NS = NT + NE - 1
    io = {"x": x, "xT": xT, "ctxT": ctxT, "out": out}
    with ExitStack() as whole:
        def sb(name, shape, dt=F32):
            return whole.enter_context(nc.sbuf_tensor(name, shape, dt))

        w = {"wqk1": sb("wqk1", [P, 2, D]), "bcol": sb("bcol", [P, 4]), "heads": sb("heads", [P, P], F32R),
             "shape_consts": sb("shape_consts_sb", [P, shape_consts.shape[1]]), "router": sb("router", [P, NE])}
        for n in ("wv1", "wo1", "wq2", "wk2", "wv2", "wo2", "bv1", "bv2", "bo1", "bo2"):
            w[n] = sb(n + "_sb", [P, D])
        cs = w["shape_consts"]
        at = [0]

        def const(n):
            at[0] += n
            return cs[:, at[0] - n:at[0]]

        w["ident"], w["same_head"], w["place"] = const(P), const(P), const(J)
        w["route_consts"] = {"earlier": const(P), "ones": const(P), "within": const(NE * NT), "rank": const(NE),
                             "ones8": const(NE), "steps": const(NT), "tile": const(NS)}
        assert at[0] == shape_consts.shape[1]
        w["qnorm"], w["knorm"] = sb("qnorm", [P, B]), sb("knorm", [P, B])
        w["x1b"] = sb("x1b", [P, B, S // P, D])
        w["x1T"] = sb("x1T", [P, B, S])
        w["logits"] = sb("logits", [P, NT, NE])
        w["x2"] = sb("x2", [P, NT, D + 4])
        w["empty"] = sb("empty", [P, D + 4])
        w["gu"] = sb("gu", [P, NE, 2 * F])
        w["down"] = sb("down_sb", [P, NE, -(-F // P), D])
        w["slots"] = nc.dram_tensor("slots", [NS * P, D + 4], F32).ap()
        loads = [(w["wqk1"][:, 0], Wq1), (w["wqk1"][:, 1], Wk1), (cs[:], shape_consts)]
        loads += [(w["bcol"][:, n:n + 1], b.rearrange("(p a) -> p a", a=1)) for n, b in enumerate((bq1, bk1, bq2, bk2))]
        loads += [(w[n][:], a) for n, a in (("wv1", Wv1), ("wo1", Wo1), ("wq2", Wq2), ("wk2", Wk2), ("wv2", Wv2), ("wo2", Wo2))]
        loads += [(w[n][:], b.rearrange("(a p) -> a p", a=1).broadcast_to([P, D]))
                  for n, b in (("bv1", bv1), ("bv2", bv2), ("bo1", bo1), ("bo2", bo2))]
        loads += [(w["router"][:], routerT)]
        w["loads"], w["n"] = loads, 16 * len(loads)
        whole_tiles = F // P * P
        w["background"] = [(w["gu"][:], gate_up)]
        w["background"] += [(w["down"][:, :, n, :], down[:, n * P:(n + 1) * P, :].rearrange("e k n -> k e n")) for n in range(F // P)]
        w["background"] += [(w["down"][0:F - whole_tiles, :, F // P, :], down[:, whole_tiles:, :].rearrange("e k n -> k e n")),
                            (w["slots"].rearrange("(s p) c -> p s c", p=P), w["empty"][:].unsqueeze(1).broadcast_to([P, NS, D + 4]))]
        w["sem"] = whole.enter_context(nc.semaphore("weights_in"))
        w["background_in"] = whole.enter_context(nc.semaphore("background_in"))
        w["empty_ready"] = whole.enter_context(nc.semaphore("empty_ready"))
        with ExitStack() as ctx:
            attention(nc, ctx, w, io)
        with ExitStack() as ctx:
            exact_attention(nc, ctx, w, io)
        with ExitStack() as ctx:
            experts(nc, ctx, w, io)


def _laid_out(x, ctx_1024, **inputs):
    import numpy as np

    plain = np.ascontiguousarray
    B, S, D = x.shape
    NE, F, _ = inputs["L0_ffn_gate_w"].shape
    NT = B * S // P
    out = {"x": plain(x), "xT": plain(x.reshape(B * S, D).T), "ctxT": plain(ctx_1024.reshape(-1, D).T)}
    for layer, tag in (("attn", "1"), ("xattn", "2")):
        for n in ("q", "k", "v", "o"):
            out["W" + n + tag] = plain(inputs[f"L0_{layer}_W{n}"])
            out["b" + n + tag] = plain(inputs[f"L0_{layer}_b{n}"])
    out["routerT"] = plain(inputs["L0_ffn_router_w"].T)
    gate_up = np.concatenate([inputs["L0_ffn_gate_w"], inputs["L0_ffn_up_w"]], axis=1)
    out["gate_up"] = plain(gate_up.transpose(2, 0, 1))
    out["down"] = plain(inputs["L0_ffn_down_w"].transpose(0, 2, 1))
    p = np.arange(P)
    parts_ = [
        np.eye(P),
        p[:, None] // E == p[None, :] // E,
        p[:, None] % 32 // E == np.arange(J)[None, :],
        p[:, None] < p[None, :],
        np.ones((P, P)),
        np.tile(np.arange(NE * NT) % NT != 0, (P, 1)),
        np.tile(np.arange(NE, 0, -1), (P, 1)),
        np.ones((P, NE)),
        np.tile(np.arange(NT) * P, (P, 1)),
        np.tile(np.arange(NT + NE - 1), (P, 1)),
    ]
    out["shape_consts"] = np.concatenate([a.astype(np.float32) for a in parts_], axis=1)
    return out


def kernel(**inputs):
    import numpy as np
    import concourse.bacc as bacc
    from concourse.bass_utils import run_bass_kernel_spmd

    nc = bacc.Bacc("TRN2", target_bir_lowering=False, num_devices=1)
    arrays = _laid_out(**{k: np.asarray(v) for k, v in inputs.items()})
    args = {n: nc.dram_tensor(n, a.shape, mybir.dt.from_np(a.dtype), kind="ExternalInput").ap() for n, a in arrays.items()}
    shape = inputs["x"].shape
    out = nc.dram_tensor("out", shape, F32, kind="ExternalOutput").ap()
    decoder_layer(nc, out=out, **args)
    r = run_bass_kernel_spmd(nc, [arrays], core_ids=[0])
    return r.results[0]["out"]
```

```python
from contextlib import ExitStack

import concourse.bass as bass
from concourse import mybir

F32 = mybir.dt.float32
F32R = mybir.dt.float32r
BF16 = mybir.dt.bfloat16
I32 = mybir.dt.int32
U32 = mybir.dt.uint32
ALU = mybir.AluOpType
ACT = mybir.ActivationFunctionType
AX = mybir.AxisListType

P = 128
LN_EPS = 1e-5
H, E = 16, 8
G, J = 4, 4
SCALE = 1.0 / float(E) ** 0.5
CEILING = 30.0
CH = 16

END = ("y2", "x2T", "lg", "ct")
PROJ = ("q2", "k2", "v2", "nq", "nk")
SELF = ("qk1", "v1", "s1", "p1T", "y1", "x1T")
TURN = ("T0", "T1", "aT")
SLOTS = {0: (("q2", "X"), ("k2", "Y")), 3: (("v2", "Y"), ("qk1", "X"), ("T0", "X")), 4: (("T1", "Y"), ("aT", "X"), ("worst", "Y")),
         5: (("s1", "Y"), ("v1", "X")), 6: (("y2", "X"),), 7: (("p1T", "Y"),), 8: (("nq", "X"),), 9: (("y1", "Y"),),
         10: (("x2T", "X"),), 11: (("nk", "Y"),), 12: (("lg", "X"),), 13: (("x1T", "Y"),), 14: (("ct", "X"),)}
ORDER = tuple(s for n in range(CH) for s in SLOTS.get(n, ()))
BANK = dict(ORDER)
SLOT = {step: n for n, steps in SLOTS.items() for step, _ in steps}
ASIDE = {"aT": 5, "x2": 8, "x1": 11, "outputs": 15}
LOOP = (2, 6)


def parts(i, B):
    return ((END if 1 <= i <= B else ()) + (PROJ if 0 <= i + 1 < B else ()) + (SELF if 0 <= i + 2 < B else ())
            + (TURN if i >= LOOP[1] else ()) + (("worst",) if i == B else ()))


def fill_numbers(B):
    at, count = {}, {"X": 0, "Y": 0}
    for i in range(-2, B + 1):
        for step, bank in ORDER:
            if step in parts(i, B):
                count[bank] += 1
                at[step, i] = count[bank]
    return at


def wait_apart(eng, w, sem, count):
    if isinstance(count, int):
        eng.wait_ge(sem, count)
        return
    eng.compute_val(count)
    eng.wait_ge(w["sem"], w["n"])
    eng.wait_ge(sem, count)


def routing_buffers(sb, QT, NE):
    r = {n: sb(n, [P, QT, NE]) for n in ("rank", "position", "mine")}
    r["chosen"] = sb("chosen", [P, QT, NE], BF16)
    r.update({n: sb(n, [P, QT]) for n in ("top", "first", "slot_f")})
    r["slot"] = sb("slot", [P, QT], U32)
    return r


def choose(V, link, r, route, logits):
    QT, NE = r["rank"].shape[1:]
    link(V.tensor_reduce(r["top"][:], logits, AX.X, ALU.max))
    for n in range(QT):
        last = V.scalar_tensor_tensor(r["rank"][:, n], logits[:, n], r["top"][:, n:n + 1], route["rank"], ALU.is_equal, ALU.mult)
    link(last)
    link(V.tensor_reduce(r["first"][:], r["rank"][:], AX.X, ALU.max))
    return V.tensor_tensor(r["chosen"][:], r["rank"][:], r["first"][:].unsqueeze(2).broadcast_to([P, QT, NE]), ALU.is_equal)


def count_chosen(mm, bank, r, w):
    NE = r["rank"].shape[2]
    first, second = r["chosen"][:, 0], r["chosen"][:, 1]
    earlier, ones = w["counting"][:, 0], w["counting"][:, 1]
    mm(bank[:, 0:NE], earlier, first)
    mm(bank[:, NE:2 * NE], earlier, second, True, False)
    mm(bank[:, NE:2 * NE], ones, first, False, True)
    mm(bank[:, 2 * NE:3 * NE], ones, first, True, False)
    return mm(bank[:, 2 * NE:3 * NE], ones, second, False, True)


def place_chosen(V, link, r, w, counts):
    QT, NE = r["rank"].shape[1:]
    link(V.tensor_tensor(r["position"][:], counts[:, 0:QT * NE].rearrange("p (t e) -> p t e", t=QT),
                         w["next_slot"][:].unsqueeze(1).broadcast_to([P, QT, NE]), ALU.add))
    link(V.tensor_tensor(w["next_slot"][:], w["next_slot"][:], counts[:, QT * NE:(QT + 1) * NE], ALU.add))
    link(V.tensor_tensor(r["mine"][:], r["position"][:], r["chosen"][:], ALU.mult))
    link(V.tensor_reduce(r["slot_f"][:], r["mine"][:], AX.X, ALU.add))
    return V.tensor_copy(r["slot"][:], r["slot_f"][:])


def list_buffers(sb, NE, NT):
    NS = NT + NE - 1
    r = {n: sb(n, [P, NE]) for n in ("tokens", "tiles", "ends", "before", "jump")}
    r.update({n: sb(n, [P, NS, NE]) for n in ("past", "jumps")})
    r.update({n: sb(n, [P, NS]) for n in ("expert_f", "jumped", "tile_f")})
    r["over"] = sb("over", [P, NE, NT])
    r["ahead"] = sb("ahead", [P, NE + 1])
    r["expert"] = sb("expert", [P, NS], I32)
    r["tile_at"] = sb("tile_at", [P, NS], I32)
    r["next_slot"] = sb("next_slot_int", [1, NE], I32)
    return r


def list_tiles(V, link, w):
    r, c = w["list"], w["route_consts"]
    NS, NE = r["past"].shape[1:]
    NT = r["over"].shape[2]
    link(V.tensor_tensor(r["tokens"][:], w["next_slot"][:], c["region"], ALU.subtract))
    V.memset(r["ahead"][:, NE:NE + 1], float(NE * (NT + 1)))
    link(V.tensor_tensor(r["over"][:], r["tokens"][:].unsqueeze(2).broadcast_to([P, NE, NT]),
                         c["steps"].unsqueeze(1).broadcast_to([P, NE, NT]), ALU.is_gt))
    link(V.tensor_reduce(r["tiles"][:], r["over"][:], AX.X, ALU.add))
    link(V.tensor_tensor_scan(r["ends"][:], c["ones8"], r["tiles"][:], 0.0, ALU.mult, ALU.add))
    link(V.tensor_tensor(r["past"][:], r["ends"][:].unsqueeze(1).broadcast_to([P, NS, NE]),
                         c["tile"].unsqueeze(2).broadcast_to([P, NS, NE]), ALU.is_le))
    link(V.tensor_reduce(r["expert_f"][:], r["past"][:], AX.X, ALU.add))
    V.tensor_scalar(r["expert"][:], r["expert_f"][:], float(NE - 1), None, ALU.min)
    link(V.tensor_tensor(r["before"][:], r["tiles"][:], r["ends"][:], ALU.subtract))
    link(V.tensor_tensor(r["ahead"][:, 0:NE], r["before"][:], c["region_tile"], ALU.add))
    link(V.tensor_tensor(r["jump"][:], r["ahead"][:, 1:NE + 1], r["ahead"][:, 0:NE], ALU.subtract))
    link(V.tensor_tensor(r["jumps"][:], r["past"][:], r["jump"][:].unsqueeze(1).broadcast_to([P, NS, NE]), ALU.mult))
    link(V.tensor_reduce(r["jumped"][:], r["jumps"][:], AX.X, ALU.add))
    link(V.scalar_tensor_tensor(r["tile_f"][:], r["jumped"][:], r["ahead"][:, 0:1], c["tile"], ALU.add, ALU.add))
    V.tensor_scalar(r["tile_at"][:], r["tile_f"][:], float(NE * (NT + 1)), None, ALU.min)


def fill_up(eng, w, experts_, tiles, filled_up):
    NE, NT = w["list"]["over"].shape[1:]
    for e in experts_:
        start = e * (NT + 1) * P
        row = eng.value_load(w["list"]["next_slot"][0:1, e:e + 1], min_val=start, max_val=start + (NT + 1 - tiles) * P)
        eng.dma_start(w["slots"][bass.ds(row, tiles * P)].rearrange("(n p) c -> p n c", p=P),
                      w["empty"][:].unsqueeze(1).broadcast_to([P, tiles, w["empty"].shape[1]])).then_inc(filled_up, 16)


ROUTE_LINKS = 7


def attention(nc, ctx, w, io):
    B, S, D = io["x"].shape
    SC = io["ctxT"].shape[1] // B
    QT, KT = S // P, SC // P
    x_t = io["x"].rearrange("b (t p) d -> b p t d", p=P)
    at = fill_numbers(B)
    lo, hi = LOOP

    def number(step, i, back=0):
        if isinstance(i, int):
            return at[step, i - back]
        first = at[step, lo - back]
        each = at[step, lo + 1] - at[step, lo]
        return first + each * (i - lo)

    for step in END + PROJ + SELF:
        for back in (0, 1):
            assert all(at[step, n - back] - at[step, lo - back] == (at[step, lo + 1] - at[step, lo]) * (n - lo)
                       for n in range(lo, hi))

    def x1T_of(b):
        return w["x1T"][:, bass.ds(b, 1)].rearrange("p b s -> p (b s)")

    def sb(name, shape, dt=F32):
        return ctx.enter_context(nc.sbuf_tensor(name, shape, dt))

    def sem(name):
        return ctx.enter_context(nc.semaphore(name))

    xTb = sb("xTb", [P, S])
    xrow = sb("xrow", [P, QT, D])
    xb = sb("xb", [P, QT, D])
    qkT1 = sb("qkT1", [P, 2, S])
    v1 = sb("v1", [P, QT, D])
    negmax1 = sb("negmax1", [P, QT])
    shift1 = sb("shift1", [P, QT])
    p1 = sb("p1", [P, QT, S])
    sum1 = sb("sum1", [P, QT])
    rsum1 = sb("rsum1", [P, QT])
    p1T = sb("p1T", [P, QT, S])
    bv_cols = sb("bv_cols", [P, P])
    wvo = sb("wvo", [P, 2, D])
    t1 = sb("t1", [P, QT, D])
    st1 = sb("st1", [P, QT, 6])
    mv1 = sb("mv1", [P, QT, 2])
    ve1 = sb("ve1", [P, QT])
    rstd1 = sb("rstd1", [P, QT])
    x1 = sb("x1", [P, QT, D])
    ctxb = sb("ctxb", [P, SC])
    qsplit = sb("qsplit", [P, 2, S], F32R)
    ksplit = sb("ksplit", [P, 2, SC], F32R)
    sq = sb("sq", [P, S], F32R)
    sk = sb("sk", [P, SC], F32R)
    kst = sb("kst", [P, 2, G, SC], F32R)
    qrep = sb("qrep", [P, G, S])
    qst = sb("qst", [P, 2, G, J, S], F32R)
    vaug = sb("vaug", [P, 2, KT, H, 32])
    NP2 = 4
    p2 = sb("p2", [P, NP2, J * S])
    oS = sb("oS", [P, G, S])
    oT = sb("oT", [P, 2, S])
    rden = sb("rden", [P, S])
    rden_rows = sb("rden_rows", [P, QT, H])
    att_rows = sb("att_rows", [P, QT, E, H])
    aT = sb("aT", [P, S])
    t2 = sb("t2", [P, QT, D])
    st2 = sb("st2", [P, QT, 6])
    mv2 = sb("mv2", [P, QT, 2])
    ve2 = sb("ve2", [P, QT])
    rstd2 = sb("rstd2", [P, QT])
    x2s = sb("x2s", [P, QT, D + 4])
    x2T = sb("x2T", [P, S])
    half = sb("half", [P, QT])
    warm = sb("warm_exp", [P, 1])
    NE = w["next_slot"].shape[1]
    r = routing_buffers(sb, QT, NE)
    qd = nc.dram_tensor("q_parts", [2, P, S], F32).ap()
    kd = nc.dram_tensor("k_parts", [2, P, SC], F32).ap()
    step_of_numbers = sb("step_of_numbers", [P, QT, 4], I32)
    od = nc.dram_tensor("outputs_and_sums", [2 * E, G, J, S], F32).ap()

    psS = ctx.enter_context(nc.psum_tensor("psS", [P, 2, J * S], F32))
    psO = ctx.enter_context(nc.psum_tensor("psO", [P, G, S], F32))
    psX = ctx.enter_context(nc.psum_tensor("psX", [P, 512], F32))
    psY = ctx.enter_context(nc.psum_tensor("psY", [P, 512], F32))
    ps = {"X": psX, "Y": psY}

    filled = {"X": sem("X_filled"), "Y": sem("Y_filled")}
    taken = {"X": sem("X_taken"), "Y": sem("Y_taken")}
    xT_in, xrow_in, ctx_in = sem("xT_in"), sem("xrow_in"), sem("ctx_in")
    xb_ready, rstd1_ready, x1b_ready, rstd2_ready = (
        sem(n) for n in ("xb_ready", "rstd1_ready", "x1b_ready", "rstd2_ready"))
    tokens_ready, routed, chosen_ready, slots_ready = (
        sem(n) for n in ("tokens_ready", "routed", "chosen_ready", "slots_ready"))
    next_ready, listed, filled_up = sem("next_slots_ready"), sem("listed"), sem("filled_up")
    half_set, rden_rows_ready = sem("half_set"), sem("rden_rows_ready")
    negmax_ready, shift_ready, rsum_ready = sem("negmax_ready"), sem("shift_ready"), sem("rsum_ready")
    t1_ready, st1_ready, mv1_ready, ve1_ready, x1_ready = (
        sem(n) for n in ("t1_ready", "st1_ready", "mv1_ready", "ve1_ready", "x1_ready"))
    t2_ready, st2_ready, mv2_ready, ve2_ready, x2_ready = (
        sem(n) for n in ("t2_ready", "st2_ready", "mv2_ready", "ve2_ready", "x2_ready"))
    qhigh_ready, khigh_ready, rden_ready = sem("qhigh_ready"), sem("khigh_ready"), sem("rden_ready")
    o_out, att_in, aT_ready = sem("outputs_out"), sem("outputs_in"), sem("aT_ready")
    bv_ready, wvo_done, wvo_ready = sem("bv_cols_ready"), sem("wvo_done"), sem("wvo_ready")
    norms_ready, worst_ready, worst_all_ready = sem("norm_products_ready"), sem("worst_ready"), sem("worst_of_all_ready")
    prod = sb("norm_products", [P, B])
    worst = sb("worst", [P, 1])
    worst_all = sb("worst_all", [1, 1])
    sq_ready, sk_ready = sem("sq_ready"), sem("sk_ready")
    heads_ready, vaug_cleared = sem("heads_ready"), sem("vaug_cleared")
    kd_in, qd_in, kst_in, qrep_in, qst_ready = (sem(n) for n in ("kd_in", "qd_in", "kst_in", "qrep_in", "qst_ready"))
    scores_done, probs_ready, pv_done, o_taken = (sem(n) for n in ("scores_done", "probs_ready", "pv_done", "o_taken"))

    block = ctx.enter_context(nc.Block())

    def rounds(eng, one):
        for i in range(-2, lo):
            one(i, i % 2, parts(i, B))
        with eng.Fori(0, (hi - lo) // 2) as r:
            for p in range(2):
                one(lo + p + 2 * r, p, parts(lo, B))
        for i in range(hi, B + 1):
            one(i, i % 2, parts(i, B))

    @block.sync
    def _(sp):
        for dst, src in w["first_loads"]:
            sp.dma_start(dst, src).then_inc(w["first_in"], 16)
        load_x = lambda b: sp.dma_start(xTb[:], io["xT"][:, bass.ds(b * S, S)]).then_inc(xT_in, 16)
        load_rows = lambda b: sp.dma_start(xrow[:], x_t[bass.ds(b, 1)].rearrange("b p t d -> p (b t) d")).then_inc(xrow_in, 16)
        load_ctx = lambda b: sp.dma_start(ctxb[:], io["ctxT"][:, bass.ds(b * SC, SC)]).then_inc(ctx_in, 16)
        load_x(0)
        load_rows(0)
        load_ctx(0)

        def one(i, p, steps):
            if "qk1" in steps and (not isinstance(i, int) or i > -2):
                sp.wait_ge(filled[BANK["v1"]], number("v1", i, 1))
                load_x(i + 2)
                if isinstance(i, int) and i < 0:
                    sp.wait_ge(xb_ready, i + 2)
                    load_rows(i + 2)
            if isinstance(i, int) and i == B:
                sp.wait_ge(next_ready, 1)
                fill_up(sp, w, range(NE // 2), QT + 1, filled_up)
            if "y2" in steps and "T0" not in steps:
                sp.wait_ge(o_taken, 2 * i)
                if not isinstance(i, int) or i > 1:
                    sp.wait_ge(att_in, 16 * (i - 1))
                for j in range(J):
                    sp.dma_start(od[:, :, j], oS[32 * j:32 * j + 2 * E]).then_inc(o_out, 16)
            if isinstance(i, int) and i == 0:
                sp.wait_ge(w["empty_ready"], 2)
                for dst, src in w["background"]:
                    sp.dma_start(dst, src).then_inc(w["background_in"], 16)
            if "k2" in steps:
                q = 1 - p
                for n in (number("k2", i), number("q2", i), 64 * (i + 1), 16 * (i + 2), CH * i, 64 * i, i - 1, number("v2", i)):
                    sp.compute_val(n)
                if not isinstance(i, int) or i >= 0:
                    sp.wait_ge(kst_in, 64 * (i + 1))
                    sp.wait_ge(qrep_in, 64 * (i + 1))
                sp.wait_ge(taken[BANK["q2"]], number("q2", i))
                sp.dma_start(qd.rearrange("c p s -> p c s"), qsplit[:].bitcast(F32)).then_inc(qd_in, 16)
                sp.wait_ge(taken[BANK["k2"]], number("k2", i))
                sp.dma_start(kd.rearrange("c p s -> p c s"), ksplit[:].bitcast(F32)).then_inc(kd_in, 16)
            if "y2" in steps and "T0" not in steps:
                sp.wait_ge(o_out, 64 * i)
                if not isinstance(i, int) or i > 1:
                    sp.wait_ge(aT_ready, i - 1)
                sp.dma_start(oT[:], od.rearrange("(n e) g j s -> (e g j) n s", n=2)).then_inc(att_in, 16)
            if "qk1" in steps and (not isinstance(i, int) or i >= 0):
                sp.wait_ge(xb_ready, i + 2)
                load_rows(i + 2)
            if "k2" in steps:
                sp.wait_ge(qd_in, 16 * (i + 2))
                if not isinstance(i, int) or i >= 0:
                    sp.wait_ge(qst_ready, i + 1)
                for c in range(4):
                    sp.dma_start(qrep[32 * c:32 * c + 32],
                                 qd[c // 2].rearrange("(g r) s -> r g s", g=G)).then_inc(qrep_in, 16)
                sp.wait_ge(kd_in, 16 * (i + 2))
                if not isinstance(i, int) or i >= 1:
                    sp.wait_ge(scores_done, CH * i)
                for c in range(4):
                    sp.dma_start(kst[32 * c:32 * c + 32, q].bitcast(F32),
                                 kd[c % 2].rearrange("(g r) s -> r g s", g=G)).then_inc(kst_in, 16)
                if not isinstance(i, int) or i + 2 < B:
                    sp.wait_ge(filled[BANK["v2"]], number("v2", i))
                    load_ctx(i + 2)
        rounds(sp, one)

    @block.tensor
    def _(pe):
        def mm(out_, l, r, start=True, stop=True, **k):
            return nc.tensor.matmul(out_, l, r, start=start, stop=stop, **k)

        def step(name, i, p):
            bank = ps[BANK[name]]
            fill = number(name, i)
            if not isinstance(fill, int) or fill > 1:
                pe.wait_ge(taken[BANK[name]], fill - 1)
            if name == "qk1":
                pe.wait_ge(xT_in, 16 * (i + 3))
                mm(bank[:, 0:S], w["wq1"], xTb[:])
                last = mm(bank[:, S:2 * S], w["wk1"], xTb[:])
            elif name == "v1":
                if isinstance(i, int) and i == -2:
                    pe.wait_ge(w["sem"], w["n"])
                    mm(psO[:, 0, 0:D], w["wv1T"], w["wo1"])
                    pe.wait_ge(bv_ready, 1)
                    mm(psO[:, 0, D:2 * D], bv_cols[:], w["wo1"]).then_inc(wvo_done, 1)
                    pe.wait_ge(wvo_ready, 1)
                for n in range(QT):
                    last = mm(bank[:, n * D:(n + 1) * D], xTb[:, n * P:(n + 1) * P], wvo[:, 0])
            elif name == "s1":
                pe.wait_ge(taken[BANK["qk1"]], number("qk1", i))
                for n in range(QT):
                    last = mm(bank[:, n * S:(n + 1) * S], qkT1[:, 0, n * P:(n + 1) * P], qkT1[:, 1, :])
            elif name == "p1T":
                for kt in range(QT):
                    for n in range(QT):
                        last = nc.tensor.transpose(bank[:, kt * S + n * P:kt * S + (n + 1) * P],
                                                   p1[:, n, kt * P:(kt + 1) * P], w["ident"])
            elif name == "y1":
                pe.wait_ge(taken[BANK["v1"]], number("v1", i))
                for n in range(QT):
                    for kt in range(QT):
                        last = mm(bank[:, n * D:(n + 1) * D], p1T[:, kt, n * P:(n + 1) * P], v1[:, kt, :], start=kt == 0, stop=kt == QT - 1)
            elif name == "x1T":
                pe.wait_ge(x1_ready, i + 3)
                for n in range(QT):
                    last = nc.tensor.transpose(bank[:, n * P:(n + 1) * P], x1[:, n, :], w["ident"])
            elif name == "q2":
                pe.wait_ge(taken[BANK["x1T"]], number("x1T", i, 1))
                last = mm(bank[:, 0:S], w["wq2"][:], x1T_of(i + 1))
            elif name == "k2":
                pe.wait_ge(ctx_in, 16 * (i + 2))
                last = mm(bank[:], w["wk2"][:], ctxb[:])
            elif name == "v2":
                for n in range(KT):
                    last = mm(bank[:, n * D:(n + 1) * D], ctxb[:, n * P:(n + 1) * P], w["wv2"][:])
            elif name == "nq":
                if isinstance(i, int) and i == -1:
                    pe.wait_ge(heads_ready, 1)
                pe.wait_ge(sq_ready, i + 2)
                last = mm(bank[:, 0:S], w["heads"][:], sq[:])
            elif name == "nk":
                pe.wait_ge(sk_ready, i + 2)
                last = mm(bank[:], w["heads"][:], sk[:])
            elif name == "y2":
                pe.wait_ge(aT_ready, i)
                for n in range(QT):
                    last = mm(bank[:, n * D:(n + 1) * D], aT[:, n * P:(n + 1) * P], w["wo2"][:])
            elif name == "x2T":
                pe.wait_ge(x2_ready, i)
                for n in range(QT):
                    last = nc.tensor.transpose(bank[:, n * P:(n + 1) * P], x2s[:, n, 0:D], w["ident"])
            elif name == "ct":
                pe.wait_ge(chosen_ready, i)
                last = count_chosen(mm, bank, r, w)
            elif name in ("T0", "T1"):
                n = int(name == "T1")
                pe.wait_ge(o_taken, 2 * i)
                for g in range(G):
                    last = nc.tensor.transpose(bank[:, g * P:(g + 1) * P], oS[:, g, n * P:(n + 1) * P], w["ident"])
            elif name == "aT":
                pe.wait_ge(taken[BANK["T1"]], number("T1", i))
                for n in range(QT):
                    last = nc.tensor.transpose(bank[:, n * P:(n + 1) * P], att_rows[:, n].rearrange("p e h -> p (e h)"), w["ident"])
            elif name == "worst":
                pe.wait_ge(worst_ready, 1)
                last = nc.tensor.transpose(bank[0:1, 0:P], worst[:], w["ident"])
            else:
                pe.wait_ge(taken[BANK["x2T"]], number("x2T", i))
                for n in range(QT):
                    last = mm(bank[:, NE * n:NE * (n + 1)], x2T[:, n * P:(n + 1) * P], w["router"][:])
            last.then_inc(filled[BANK[name]], 1)

        def scores(i, p, c):
            g, kt = c // KT, c % KT
            if c == 0:
                pe.wait_ge(kst_in, 64 * (i + 1))
                pe.wait_ge(qst_ready, i + 1)
            if c >= 2 or not isinstance(i, int) or i > 0:
                pe.wait_ge(probs_ready, CH * i + c - 1)
            for jj in range(J // 2):
                last = mm(psS[:, c % 2, jj * 2 * S:(jj + 1) * 2 * S], kst[:, p, g, kt * P:(kt + 1) * P],
                          qst[:, p, g, 2 * jj:2 * jj + 2, :])
            last.then_inc(scores_done, 1)

        def times_v(i, p, c):
            g, kt = c // KT, c % KT
            if c % 8 == 0 and (not isinstance(i, int) or i > 0):
                pe.wait_ge(o_taken, 2 * i - 1 + c // 8)
            pe.wait_ge(probs_ready, CH * i + c + 1)
            for j in range(J):
                last = mm(psO[32 * j:32 * j + 32, g, :], vaug[:, p, kt, G * g + j, :], p2[:, c % NP2, j * S:(j + 1) * S],
                          start=kt == 0, stop=kt == KT - 1, tile_position=(0, 32 * j), skip_group_check=True)
            last.then_inc(pv_done, 1)

        def one(i, p, steps):
            cross = not isinstance(i, int) or 0 <= i < B
            for c in range(CH):
                if cross and c + 1 < CH:
                    scores(i, p, c + 1)
                if cross and c == CH - 1 and "k2" in steps:
                    scores(i + 1, 1 - p, 0)
                for name, _ in SLOTS.get(c, ()):
                    if name in steps:
                        step(name, i, p)
                if cross:
                    times_v(i, p, c)
            if isinstance(i, int) and i == -1:
                pe.wait_ge(vaug_cleared, 2)
                scores(0, 0, 0)

        pe.wait_ge(w["first_in"], 16 * len(w["first_loads"]))
        rounds(pe, one)

    @block.scalar
    def _(act):
        def one(i, p, steps):
            cross = not isinstance(i, int) or 0 <= i < B
            for c in range(CH):
                if cross:
                    act.wait_ge(scores_done, CH * i + c + 1)
                    if c >= NP2 or not isinstance(i, int) or i > 0:
                        act.wait_ge(pv_done, CH * i + c + 1 - NP2)
                    nc.scalar.activation(p2[:, c % NP2, :], psS[:, c % 2, :], ACT.Exp, scale=SCALE,
                                         bias=-CEILING).then_inc(probs_ready, 1)
                if c == SLOT["qk1"] + 1 and "qk1" in steps:
                    bank = ps[BANK["qk1"]]
                    act.wait_ge(filled[BANK["qk1"]], number("qk1", i))
                    nc.scalar.activation(qkT1[:, 0, :], bank[:, 0:S], ACT.Identity, bias=w["bcol"][:, 0:1])
                    nc.scalar.activation(qkT1[:, 1, :], bank[:, S:2 * S], ACT.Identity,
                                         bias=w["bcol"][:, 1:2]).then_inc(taken[BANK["qk1"]], 1)
                    if isinstance(i, int) and i == -2:
                        act.wait_ge(wvo_done, 1)
                        nc.scalar.activation(wvo[:].rearrange("p n d -> p (n d)"), psO[:, 0, 0:2 * D], ACT.Identity).then_inc(wvo_ready, 1)
                if c == SLOT["s1"] + 1 and "s1" in steps:
                    act.wait_ge(shift_ready, i + 3)
                    for n in range(QT):
                        last = nc.scalar.activation(p1[:, n, :], ps[BANK["s1"]][:, n * S:(n + 1) * S], ACT.Exp, scale=SCALE,
                                                    bias=shift1[:, n:n + 1], accum_out=sum1[:, n:n + 1])
                    last.then_inc(taken[BANK["s1"]], 1)

        for dst, src in w["loads"]:
            act.dma_start(dst, src).then_inc(w["sem"], 16)
        act.wait_ge(half_set, 1)
        nc.scalar.activation(warm[:], half[:, 0:1], ACT.Exp)
        act.wait_ge(w["first_in"], 16 * len(w["first_loads"]))
        rounds(act, one)
        act.wait_ge(next_ready, 1)
        act.wait_ge(w["empty_ready"], 2)
        fill_up(act, w, range(NE // 2, NE), QT + 1, filled_up)

    @block.vector
    def _(dve):
        V = nc.vector

        def read(name, i):
            dve.wait_ge(filled[BANK[name]], number(name, i))
            return ps[BANK[name]]

        def took(name, ins):
            ins.then_inc(taken[BANK[name]], 1)

        def split(name, i, dst, n, bias, high_ready):
            bank = read(name, i)
            V.tensor_scalar(dst[:, 0, :], bank[:, 0:n], bias, None, ALU.add).then_inc(high_ready, 1)
            dve.wait_ge(high_ready, i + 2)
            took(name, V.scalar_tensor_tensor(dst[:, 1, :], bank[:, 0:n], bias, dst[:, 0, :].bitcast(F32),
                                              ALU.add, ALU.subtract))

        def statistics(src, src_ready, st, st_ready, mv, mv_ready, ve, ve_ready, count):
            dve.wait_ge(src_ready, count)
            for n in range(QT):
                last = V.bn_stats(st[:, n, :], src[:, n, :])
            last.then_inc(st_ready, 1)
            wait_apart(dve, w, st_ready, count)
            for n in range(QT):
                last = V.bn_aggr(mv[:, n, :], st[:, n, :])
            last.then_inc(mv_ready, 1)
            dve.wait_ge(mv_ready, count)
            V.tensor_scalar(ve[:], mv[:, :, 1], LN_EPS, None, ALU.add).then_inc(ve_ready, 1)

        def outputs(half, count):
            dve.wait_ge(pv_done, count)
            V.tensor_copy(oS[:, 2 * half:2 * half + 2], psO[:, 2 * half:2 * half + 2]).then_inc(o_taken, 1)

        def step(name, i, p):
            if name == "k2":
                if not isinstance(i, int) or i >= 0:
                    dve.wait_ge(kd_in, 16 * (i + 1))
                    dve.wait_ge(sk_ready, i + 1)
                split("k2", i, ksplit, SC, w["bcol"][:, 3:4], khigh_ready)
            elif name == "q2":
                if not isinstance(i, int) or i >= 0:
                    dve.wait_ge(qd_in, 16 * (i + 1))
                    dve.wait_ge(sq_ready, i + 1)
                split("q2", i, qsplit, S, w["bcol"][:, 2:3], qhigh_ready)
            elif name == "v2":
                if not isinstance(i, int) or i > 0:
                    dve.wait_ge(pv_done, CH * i)
                bank = read(name, i)
                took(name, V.tensor_tensor(vaug[:, 1 - p, :, :, 0:E], bank[:].rearrange("p (t h e) -> p t h e", t=KT, h=H),
                                           w["bv2"][:].rearrange("p (h e) -> p h e", h=H).unsqueeze(1).broadcast_to([P, KT, H, E]),
                                           ALU.add))
            elif name == "v1":
                took(name, V.tensor_tensor(v1[:], read(name, i)[:, 0:QT * D].rearrange("p (t d) -> p t d", t=QT),
                                           wvo[:, 1:2].broadcast_to([P, QT, D]), ALU.add))
            elif name == "y2":
                bank = read(name, i)
                dve.wait_ge(x1b_ready, i)
                V.tensor_tensor(t2[:], bank[:, 0:QT * D].rearrange("p (t d) -> p t d", t=QT), x1b_of(i - 1), ALU.add).then_inc(t2_ready, 1)
                dve.wait_ge(t2_ready, i)
                dve.sem_inc(taken[BANK[name]], 1)
                statistics(t2, t2_ready, st2, st2_ready, mv2, mv2_ready, ve2, ve2_ready, i)
            elif name == "s1":
                bank = read(name, i)
                V.tensor_reduce(negmax1[:], bank[:].rearrange("p (t k) -> p t k", t=QT), AX.X, ALU.max,
                                negate=True).then_inc(negmax_ready, 1)
                dve.wait_ge(negmax_ready, i + 3)
                V.tensor_scalar(shift1[:], negmax1[:], SCALE, None, ALU.mult).then_inc(shift_ready, 1)
            elif name == "nq":
                took(name, V.tensor_reduce(w["qnorm"][:, bass.ds(i + 1, 1)], read(name, i)[:, 0:S], AX.X, ALU.max))
            elif name == "nk":
                took(name, V.tensor_reduce(w["knorm"][:, bass.ds(i + 1, 1)], read(name, i)[:], AX.X, ALU.max))
            elif name == "p1T":
                bank = read(name, i)
                V.reciprocal(rsum1[:], sum1[:]).then_inc(rsum_ready, 1)
                took(name, V.tensor_copy(p1T[:].rearrange("p t d -> p (t d)"), bank[:]))
            elif name == "x2T":
                took(name, V.tensor_copy(x2T[:], read(name, i)[:, 0:S]))
            elif name == "y1":
                bank = read(name, i)
                dve.wait_ge(xb_ready, i + 3)
                dve.wait_ge(rsum_ready, i + 3)
                for n in range(QT):
                    last = V.scalar_tensor_tensor(t1[:, n, :], bank[:, n * D:(n + 1) * D], rsum1[:, n:n + 1], xb[:, n, :],
                                                  ALU.mult, ALU.add)
                last.then_inc(t1_ready, 1)
                dve.wait_ge(t1_ready, i + 3)
                dve.sem_inc(taken[BANK[name]], 1)
                statistics(t1, t1_ready, st1, st1_ready, mv1, mv1_ready, ve1, ve1_ready, i + 3)
            elif name in ("T0", "T1"):
                n = int(name == "T1")
                T = read(name, i)[:].rearrange("p (h c) -> p h c", c=32)
                V.reciprocal(rden_rows[:, n, :], T[:, :, E]).then_inc(rden_rows_ready, 1)
                dve.wait_ge(rden_rows_ready, 2 * (i - hi) + n + 1)
                took(name, V.tensor_tensor(att_rows[:, n].rearrange("p e h -> p h e"), T[:, :, 0:E],
                                           rden_rows[:, n, :].unsqueeze(2).broadcast_to([P, H, E]), ALU.mult))
            elif name == "aT":
                V.tensor_copy(aT[:], read(name, i)[:, 0:S]).then_inc(aT_ready, 1)
                dve.wait_ge(aT_ready, i)
                dve.sem_inc(taken[BANK[name]], 1)
            elif name == "worst":
                bank = read(name, i)
                V.tensor_reduce(worst_all[:], bank[0:1, 0:P], AX.X, ALU.max).then_inc(worst_all_ready, 1)
                dve.wait_ge(worst_all_ready, 1)
                dve.sem_inc(taken[BANK[name]], 1)
                V.tensor_scalar(w["unbounded"][:], worst_all[:], 0.98 * (CEILING / SCALE) ** 2, 0.0,
                                ALU.is_le, ALU.is_equal).then_inc(w["decided"], 1)
            elif name in ("lg", "ct"):
                links = [0 if name == "lg" else 3]

                def link(ins):
                    links[0] += 1
                    ins.then_inc(routed, 1)
                    dve.wait_ge(routed, ROUTE_LINKS * (i - 1) + links[0])

                bank = read(name, i)
                if name == "lg":
                    choose(V, link, r, w["route_consts"], bank[:, 0:NE * QT].rearrange("p (t e) -> p t e", t=QT)).then_inc(chosen_ready, 1)
                    dve.sem_inc(taken[BANK[name]], 1)
                else:
                    if not isinstance(i, int) or i > 1:
                        dve.wait_ge(w["scattered"], 32 * (i - 1))
                    place_chosen(V, link, r, w, bank).then_inc(slots_ready, 1)
                    dve.sem_inc(taken[BANK[name]], 1)
                    if isinstance(i, int) and i == B - 1:
                        V.tensor_copy(w["list"]["next_slot"][:], w["next_slot"][0:1]).then_inc(next_ready, 1)
                    assert links[0] == ROUTE_LINKS
            elif name == "x1T":
                took(name, V.tensor_copy(x1T_of(i + 2), read(name, i)[:, 0:S]))

        def x1b_of(b):
            return w["x1b"][:, bass.ds(b, 1)].rearrange("p b t d -> p (b t) d")

        def one(i, p, steps):
            cross = not isinstance(i, int) or 0 <= i < B
            if not isinstance(i, int) or i >= 1:
                outputs(1, CH * i)
            if isinstance(i, int) and i == B:
                V.tensor_tensor(prod[:], w["qnorm"][:], w["knorm"][:], ALU.mult).then_inc(norms_ready, 1)
                dve.wait_ge(norms_ready, 1)
                V.tensor_reduce(worst[:], prod[:], AX.X, ALU.max).then_inc(worst_ready, 1)
            for c in range(CH):
                if c == ASIDE["aT"] and "y2" in steps and "T0" not in steps:
                    dve.wait_ge(att_in, 16 * i)
                    V.reciprocal(rden[:], oT[:, 1]).then_inc(rden_ready, 1)
                    dve.wait_ge(rden_ready, i)
                    V.tensor_tensor(aT[:], oT[:, 0], rden[:], ALU.mult).then_inc(aT_ready, 1)
                for name, _ in SLOTS.get(c, ()):
                    if name in steps and name != "qk1":
                        step(name, i, p)
                if c == ASIDE["x1"] and "x1T" in steps:
                    dve.wait_ge(rstd1_ready, i + 3)
                    if not isinstance(i, int) or i > -2:
                        dve.wait_ge(x1b_ready, i + 2)
                    for n in range(QT):
                        last = V.tensor_scalar(x1[:, n, :], t1[:, n, :], mv1[:, n, 0:1], rstd1[:, n:n + 1], ALU.subtract, ALU.mult)
                    last.then_inc(x1_ready, 1)
                if c == ASIDE["x2"] and "y2" in steps:
                    dve.wait_ge(rstd2_ready, i)
                    if not isinstance(i, int) or i >= 2:
                        dve.wait_ge(w["scattered"], 32 * (i - 1))
                    for n in range(QT):
                        last = V.tensor_scalar(x2s[:, n, 0:D], t2[:, n, :], mv2[:, n, 0:1], rstd2[:, n:n + 1], ALU.subtract, ALU.mult)
                    last.then_inc(x2_ready, 1)
                if c == ASIDE["outputs"] and cross:
                    if "T0" not in steps and (not isinstance(i, int) or i >= 1):
                        dve.wait_ge(o_out, 64 * i)
                    outputs(0, CH * i + 8)

        dve.wait_ge(w["sem"], w["n"])
        dve.wait_ge(w["first_in"], 16 * len(w["first_loads"]))
        V.tensor_scalar(bv_cols[:], w["route_consts"]["ones"], w["bcol"][:, 4:5], None, ALU.mult).then_inc(bv_ready, 1)
        V.tensor_copy(w["heads"][:], w["same_head"]).then_inc(heads_ready, 1)
        V.tensor_copy(w["counting"][:, 0], w["route_consts"]["earlier"])
        V.tensor_copy(w["counting"][:, 1], w["route_consts"]["ones"])
        V.tensor_copy(w["next_slot"][:], w["route_consts"]["region"])
        rounds(dve, one)
        steps = [0]

        def link(ins):
            steps[0] += 1
            ins.then_inc(listed, 1)
            dve.wait_ge(listed, steps[0])

        list_tiles(V, link, w)

    @block.gpsimd
    def _(pool):
        Q = nc.gpsimd

        def one(i, p, steps):
            if "qk1" in steps:
                pool.wait_ge(xrow_in, 16 * (i + 3))
                if not isinstance(i, int) or i > -2:
                    pool.wait_ge(t1_ready, i + 2)
                Q.tensor_tensor(xb[:], xrow[:], w["bo1"][:].unsqueeze(1).broadcast_to([P, QT, D]), ALU.add).then_inc(xb_ready, 1)
            if "k2" in steps:
                if not isinstance(i, int) or i >= 0:
                    for name in ("nq", "nk"):
                        pool.wait_ge(filled[BANK[name]], number(name, i, 1))
                pool.wait_ge(khigh_ready, i + 2)
                Q.tensor_tensor(sk[:], ksplit[:, 0, :].bitcast(F32), ksplit[:, 0, :].bitcast(F32), ALU.mult).then_inc(sk_ready, 1)
                pool.wait_ge(qhigh_ready, i + 2)
                Q.tensor_tensor(sq[:], qsplit[:, 0, :].bitcast(F32), qsplit[:, 0, :].bitcast(F32), ALU.mult).then_inc(sq_ready, 1)
            if "y2" in steps:
                if not isinstance(i, int) or i > 1:
                    pool.wait_ge(w["scattered"], 32 * (i - 1))
                    Q.tensor_tensor(numbers, numbers, step_of_numbers[:], ALU.add).then_inc(tokens_ready, 1)
                pool.wait_ge(ve2_ready, i)
                Q.tensor_tensor(rstd2[:], ve2[:], half[:], ALU.pow).then_inc(rstd2_ready, 1)
            if "k2" in steps:
                pool.wait_ge(qrep_in, 64 * (i + 2))
                if not isinstance(i, int) or i >= 1:
                    wait_apart(pool, w, scores_done, CH * i)
                for j in range(J):
                    last = Q.tensor_scalar(qst[:, 1 - p, :, j, :], qrep[:], w["place"][:, j:j + 1], 1.0, ALU.mult, ALU.mult)
                last.then_inc(qst_ready, 1)
            if "qk1" in steps:
                pool.wait_ge(ve1_ready, i + 3)
                Q.tensor_tensor(rstd1[:], ve1[:], half[:], ALU.pow).then_inc(rstd1_ready, 1)
                pool.wait_ge(x1_ready, i + 3)
                Q.tensor_tensor(x1b_of(i + 2), x1[:], w["bo2"][:].unsqueeze(1).broadcast_to([P, QT, D]), ALU.add).then_inc(x1b_ready, 1)
            if "y2" in steps:
                if isinstance(i, int) and i == B:
                    pool.wait_ge(filled_up, 16 * NE)
                wait_apart(pool, w, slots_ready, i)
                pool.wait_ge(tokens_ready, i)
                pool.wait_ge(x2_ready, i)
                for n in range(QT):
                    Q.indirect_dma_start(out=w["slots"], out_offset=bass.IndirectOffsetOnAxis(ap=r["slot"][:, n:n + 1], axis=0),
                                         in_=x2s[:, n, :], in_offset=None).then_inc(w["scattered"], 16)

        def x1b_of(b):
            return w["x1b"][:, bass.ds(b, 1)].rearrange("p b t d -> p (b t) d")

        Q.memset(half[:], -0.5).then_inc(half_set, 1)
        Q.memset(vaug[:, :, :, :, 2 * E:32], 0.0).then_inc(vaug_cleared, 1)
        Q.memset(vaug[:, :, :, :, E:2 * E], 1.0).then_inc(vaug_cleared, 1)
        Q.memset(w["empty"][:, 0:D], 0.0).then_inc(w["empty_ready"], 1)
        Q.iota(w["empty"][:, D:D + 4].bitcast(I32), [[0, 4]], base=B * S, channel_multiplier=1).then_inc(w["empty_ready"], 1)
        numbers = x2s[:, :, D:D + 4].bitcast(I32)
        Q.iota(numbers, [[P, QT], [0, 4]], base=0, channel_multiplier=1).then_inc(tokens_ready, 1)
        Q.iota(step_of_numbers[:], [[0, QT], [0, 4]], base=S, channel_multiplier=0)
        pool.wait_ge(w["sem"], w["n"])
        rounds(pool, one)
        pool.wait_ge(w["scattered"], 32 * B)


def exact_attention(nc, ctx, w, io):
    B, S, D = io["x"].shape
    SC = io["ctxT"].shape[1] // B
    QT, KT = S // P, SC // P
    CHUNKS, MAXIMA = G * KT, H * QT

    def sb(name, shape, dt=F32):
        return ctx.enter_context(nc.sbuf_tensor(name, shape, dt))

    def sem(name):
        return ctx.enter_context(nc.semaphore("e_" + name))

    ctxb = sb("e_ctxb", [P, SC])
    qsplit = sb("e_qsplit", [P, 2, S], F32R)
    ksplit = sb("e_ksplit", [P, 2, SC], F32R)
    kst = sb("e_kst", [P, G, SC], F32R)
    qst = sb("e_qst", [P, G, J, S], F32R)
    vaug = sb("e_vaug", [P, KT, H, 32])
    m2 = sb("e_maxima", [P, QT, J, G])
    msplit = sb("e_msplit", [H, 2, S], F32R)
    p2 = sb("e_p2", [P, 2, J * S])
    oS = sb("e_oS", [P, G, S])
    rden = sb("e_rden", [P, QT, H])
    att = sb("e_att", [P, QT, E, H])
    aT = sb("e_aT", [P, S])
    t2 = sb("e_t2", [P, QT, D])
    st2 = sb("e_st2", [P, QT, 6])
    mv2 = sb("e_mv2", [P, QT, 2])
    ve2 = sb("e_ve2", [P, QT])
    rstd2 = sb("e_rstd2", [P, QT])
    x2s = sb("e_x2s", [P, QT, D + 4])
    numbers = x2s[:, :, D:D + 4].bitcast(I32)
    step_of_numbers = sb("e_step_of_numbers", [P, QT, 4], I32)
    NE = w["next_slot"].shape[1]
    r = routing_buffers(lambda name, shape, dt=F32: sb("e_" + name, shape, dt), QT, NE)
    x2T = sb("e_x2T", [P, S])
    half = sb("e_half", [P, QT])
    qd = nc.dram_tensor("e_q_parts", [2, P, S], F32).ap()
    kd = nc.dram_tensor("e_k_parts", [2, P, SC], F32).ap()
    md = nc.dram_tensor("e_m_parts", [H, 2, S], F32).ap()
    psS = ctx.enter_context(nc.psum_tensor("e_psS", [P, 2, J * S], F32))
    psO = ctx.enter_context(nc.psum_tensor("e_psO", [P, G, S], F32))
    psX = ctx.enter_context(nc.psum_tensor("e_psX", [P, 512], F32))
    psY = ctx.enter_context(nc.psum_tensor("e_psY", [P, 512], F32))

    vaug_cleared, start = sem("vaug_cleared"), sem("batch_may_start")
    names = ("q2", "k2", "v2", "mT", "T0", "T1", "aT", "y2", "x2T", "lg", "ct")
    done = {n: sem(n + "_done") for n in names}
    took = {n: sem(n + "_taken") for n in names}
    ctx_in, kd_in, qd_in, md_in = sem("ctx_in"), sem("k_parts_out"), sem("q_parts_out"), sem("m_parts_out")
    kst_in, qst_in, mst_in = sem("kst_in"), sem("qst_in"), sem("m_rows_in")
    max_done, max_taken, scores_done, probs_ready, pv_done = (
        sem(n) for n in ("max_scores_done", "maximum_taken", "scores_done", "probs_ready", "pv_done"))
    o_taken, ve2_ready, rstd2_ready, x2_ready, step_done = (
        sem(n) for n in ("o_taken", "ve2_ready", "rstd2_ready", "x2_ready", "dve_step_done"))
    tokens_ready, chosen_ready, slots_ready = sem("tokens_ready"), sem("chosen_ready"), sem("slots_ready")
    next_ready, listed, filled_up = sem("next_slots_ready"), sem("listed"), sem("filled_up")
    CLEARED = 7

    def for_batches(eng, one, prepare=lambda: None, finish=lambda: None):
        eng.wait_ge(w["decided"], 1)
        flag = eng.value_load(w["unbounded"][0:1, 0:1], min_val=0, max_val=1)
        with eng.If(flag > 0):
            prepare()
            with eng.Fori(0, B) as b:
                eng.wait_ge(start, b + CLEARED)
                one(b)
            eng.wait_ge(start, B + CLEARED)
            finish()

    block = ctx.enter_context(nc.Block())

    @block.sync
    def _(sp):
        def one(b):
            sp.dma_start(ctxb[:], io["ctxT"][:, bass.ds(b * SC, SC)]).then_inc(ctx_in, 16)
            sp.wait_ge(took["k2"], b + 1)
            sp.dma_start(kd.rearrange("c p s -> p c s"), ksplit[:].bitcast(F32)).then_inc(kd_in, 16)
            sp.wait_ge(took["q2"], b + 1)
            sp.dma_start(qd.rearrange("c p s -> p c s"), qsplit[:].bitcast(F32)).then_inc(qd_in, 16)
            sp.wait_ge(kd_in, 16 * (b + 1))
            for c, part in enumerate((0, 1, 0)):
                sp.dma_start(kst[32 * c:32 * c + 32].bitcast(F32), kd[part].rearrange("(g r) s -> r g s", g=G)).then_inc(kst_in, 16)
            sp.wait_ge(qd_in, 16 * (b + 1))
            for c, part in enumerate((0, 0, 1)):
                for j in range(J):
                    r = 32 * c + E * j
                    sp.dma_start(qst[r:r + E, :, j, :].bitcast(F32),
                                 qd[part].rearrange("(g r) s -> r g s", g=G)[E * j:E * j + E]).then_inc(qst_in, 16)
            sp.wait_ge(took["mT"], b + 1)
            sp.dma_start(md, msplit[:].bitcast(F32)).then_inc(md_in, 16)
            sp.wait_ge(md_in, 16 * (b + 1))
            for j in range(J):
                r = 96 + E * j
                sp.dma_start(qst[r:r + 2, :, j, :].bitcast(F32),
                             md[G * j:G * j + G].rearrange("g r s -> r g s")).then_inc(mst_in, 16)

        def finish():
            sp.wait_ge(next_ready, 1)
            fill_up(sp, w, range(NE), 1, filled_up)
            sp.wait_ge(filled_up, 16 * NE)

        for_batches(sp, one, finish=finish)

    @block.tensor
    def _(pe):
        def mm(out_, l, r, start_=True, stop=True, **k):
            return nc.tensor.matmul(out_, l, r, start=start_, stop=stop, **k)

        def one(b):
            x1T_b = w["x1T"][:, bass.ds(b, 1)].rearrange("p b s -> p (b s)")
            pe.wait_ge(ctx_in, 16 * (b + 1))
            mm(psY[:], w["wk2"][:], ctxb[:]).then_inc(done["k2"], 1)
            mm(psX[:, 0:S], w["wq2"][:], x1T_b).then_inc(done["q2"], 1)
            pe.wait_ge(took["q2"], b + 1)
            for t in range(KT):
                last = mm(psX[:, t * D:(t + 1) * D], ctxb[:, t * P:(t + 1) * P], w["wv2"][:])
            last.then_inc(done["v2"], 1)
            pe.wait_ge(took["k2"], b + 1)
            pe.wait_ge(took["v2"], b + 1)
            pe.wait_ge(kst_in, 48 * (b + 1))
            pe.wait_ge(qst_in, 192 * (b + 1))
            for n in range(MAXIMA):
                g, j, t = n // (J * QT), n // QT % J, n % QT
                if n >= 2:
                    pe.wait_ge(max_taken, MAXIMA * b + n - 1)
                mm((psY, psX)[n % 2][:], qst[0:96, g, j, t * P:(t + 1) * P], kst[0:96, g, :]).then_inc(max_done, 1)
            pe.wait_ge(max_taken, MAXIMA * (b + 1))
            for t in range(QT):
                last = nc.tensor.transpose(psY[0:H, t * P:(t + 1) * P], m2[:, t].rearrange("p j g -> p (j g)"), w["ident"])
            last.then_inc(done["mT"], 1)
            pe.wait_ge(mst_in, 64 * (b + 1))
            for c in range(CHUNKS):
                g, kt = c // KT, c % KT
                if c >= 2:
                    pe.wait_ge(probs_ready, CHUNKS * b + c - 1)
                for jj in range(J // 2):
                    last = mm(psS[:, c % 2, jj * 2 * S:(jj + 1) * 2 * S], kst[:, g, kt * P:(kt + 1) * P], qst[:, g, 2 * jj:2 * jj + 2, :])
                last.then_inc(scores_done, 1)
                pe.wait_ge(probs_ready, CHUNKS * b + c + 1)
                for j in range(J):
                    last = mm(psO[32 * j:32 * j + 32, g, :], vaug[:, kt, G * g + j, :], p2[:, c % 2, j * S:(j + 1) * S],
                              start_=kt == 0, stop=kt == KT - 1, tile_position=(0, 32 * j), skip_group_check=True)
                last.then_inc(pv_done, 1)
            pe.wait_ge(o_taken, b + 1)
            for n, (name, bank) in enumerate((("T0", psX), ("T1", psY))):
                for g in range(G):
                    last = nc.tensor.transpose(bank[:, g * P:(g + 1) * P], oS[:, g, n * P:(n + 1) * P], w["ident"])
                last.then_inc(done[name], 1)
            pe.wait_ge(took["T1"], b + 1)
            for n in range(QT):
                last = nc.tensor.transpose(psX[:, n * P:(n + 1) * P], att[:, n].rearrange("p e h -> p (e h)"), w["ident"])
            last.then_inc(done["aT"], 1)
            pe.wait_ge(took["aT"], b + 1)
            for n in range(QT):
                last = mm(psY[:, n * D:(n + 1) * D], aT[:, n * P:(n + 1) * P], w["wo2"][:])
            last.then_inc(done["y2"], 1)
            pe.wait_ge(x2_ready, b + 1)
            for n in range(QT):
                last = nc.tensor.transpose(psX[:, n * P:(n + 1) * P], x2s[:, n, 0:D], w["ident"])
            last.then_inc(done["x2T"], 1)
            pe.wait_ge(took["x2T"], b + 1)
            for n in range(QT):
                last = mm(psY[:, NE * n:NE * (n + 1)], x2T[:, n * P:(n + 1) * P], w["router"][:])
            last.then_inc(done["lg"], 1)
            pe.wait_ge(chosen_ready, b + 1)
            count_chosen(mm, psX, r, w).then_inc(done["ct"], 1)

        for_batches(pe, one)

    @block.scalar
    def _(act):
        def one(b):
            for c in range(CHUNKS):
                if c >= 2:
                    act.wait_ge(pv_done, CHUNKS * b + c - 1)
                act.wait_ge(scores_done, CHUNKS * b + c + 1)
                nc.scalar.activation(p2[:, c % 2, :], psS[:, c % 2, :], ACT.Exp, scale=SCALE).then_inc(probs_ready, 1)

        for_batches(act, one)

    @block.vector
    def _(dve):
        V = nc.vector
        def prepare():
            V.memset(kst[96:128].rearrange("p g s -> p (g s)").bitcast(F32), 1.0).then_inc(start, 1)
            V.memset(qst[:].rearrange("p g j s -> p (g j s)").bitcast(F32), 0.0).then_inc(start, 1)
            V.tensor_copy(w["next_slot"][:], w["route_consts"]["region"]).then_inc(start, 1)

        LINKS = 8 + ROUTE_LINKS

        def one(b):
            links = [0]

            def link(ins):
                links[0] += 1
                ins.then_inc(step_done, 1)
                wait_apart(dve, w, step_done, LINKS * b + links[0])

            def read(name, bank):
                dve.wait_ge(done[name], b + 1)
                return bank

            def split(name, dst, bank, n, bias):
                read(name, bank)
                link(V.tensor_scalar(dst[:, 0, :], bank[:, 0:n], bias, None, ALU.add))
                V.scalar_tensor_tensor(dst[:, 1, :], bank[:, 0:n], bias, dst[:, 0, :].bitcast(F32),
                                       ALU.add, ALU.subtract).then_inc(took[name], 1)

            split("k2", ksplit, psY, SC, w["bcol"][:, 3:4])
            split("q2", qsplit, psX, S, w["bcol"][:, 2:3])
            V.tensor_tensor(vaug[:, :, :, 0:E], read("v2", psX)[:].rearrange("p (t h e) -> p t h e", t=KT, h=H),
                            w["bv2"][:].rearrange("p (h e) -> p h e", h=H).unsqueeze(1).broadcast_to([P, KT, H, E]),
                            ALU.add).then_inc(took["v2"], 1)
            for n in range(MAXIMA):
                g, j, t = n // (J * QT), n // QT % J, n % QT
                dve.wait_ge(max_done, MAXIMA * b + n + 1)
                V.tensor_reduce(m2[:, t, j, g:g + 1], (psY, psX)[n % 2][:], AX.X, ALU.max).then_inc(max_taken, 1)
            read("mT", psY)
            link(V.tensor_scalar(msplit[:, 0, :], psY[0:H, 0:S], -1.0, None, ALU.mult))
            V.scalar_tensor_tensor(msplit[:, 1, :], psY[0:H, 0:S], -1.0, msplit[:, 0, :].bitcast(F32),
                                   ALU.mult, ALU.subtract).then_inc(took["mT"], 1)
            dve.wait_ge(pv_done, CHUNKS * (b + 1))
            V.tensor_copy(oS[:], psO[:]).then_inc(o_taken, 1)
            for n, (name, bank) in enumerate((("T0", psX), ("T1", psY))):
                T = read(name, bank)[:].rearrange("p (h c) -> p h c", c=32)
                link(V.reciprocal(rden[:, n, :], T[:, :, E]))
                V.tensor_tensor(att[:, n].rearrange("p e h -> p h e"), T[:, :, 0:E], rden[:, n, :].unsqueeze(2).broadcast_to([P, H, E]),
                                ALU.mult).then_inc(took[name], 1)
            V.tensor_copy(aT[:], read("aT", psX)[:, 0:S]).then_inc(took["aT"], 1)
            link(V.tensor_tensor(t2[:], read("y2", psY)[:, 0:QT * D].rearrange("p (t d) -> p t d", t=QT),
                                 w["x1b"][:, bass.ds(b, 1)].rearrange("p b t d -> p (b t) d"), ALU.add))
            for n in range(QT):
                last = V.bn_stats(st2[:, n, :], t2[:, n, :])
            link(last)
            for n in range(QT):
                last = V.bn_aggr(mv2[:, n, :], st2[:, n, :])
            link(last)
            V.tensor_scalar(ve2[:], mv2[:, :, 1], LN_EPS, None, ALU.add).then_inc(ve2_ready, 1)
            dve.wait_ge(rstd2_ready, b + 1)
            for n in range(QT):
                last = V.tensor_scalar(x2s[:, n, 0:D], t2[:, n, :], mv2[:, n, 0:1], rstd2[:, n:n + 1], ALU.subtract, ALU.mult)
            last.then_inc(x2_ready, 1)
            V.tensor_copy(x2T[:], read("x2T", psX)[:, 0:S]).then_inc(took["x2T"], 1)
            choose(V, link, r, w["route_consts"],
                   read("lg", psY)[:, 0:NE * QT].rearrange("p (t e) -> p t e", t=QT)).then_inc(chosen_ready, 1)
            place_chosen(V, link, r, w, read("ct", psX)).then_inc(slots_ready, 1)
            assert links[0] == LINKS
            dve.wait_ge(w["scattered"], 32 * (b + 1 + B))
            dve.sem_inc(start, 1)

        def finish():
            V.tensor_copy(w["list"]["next_slot"][:], w["next_slot"][0:1]).then_inc(next_ready, 1)
            steps = [0]

            def link(ins):
                steps[0] += 1
                ins.then_inc(listed, 1)
                dve.wait_ge(listed, steps[0])

            list_tiles(V, link, w)

        for_batches(dve, one, prepare, finish)

    @block.gpsimd
    def _(pool):
        Q = nc.gpsimd
        def prepare():
            Q.memset(vaug[:, :, :, E:32], 0.0).then_inc(vaug_cleared, 1)
            pool.wait_ge(vaug_cleared, 1)
            Q.memset(vaug[:, :, :, E:E + 1], 1.0).then_inc(start, 1)
            Q.memset(half[:], -0.5).then_inc(start, 1)
            Q.iota(numbers, [[P, QT], [0, 4]], base=-S, channel_multiplier=1).then_inc(start, 1)
            Q.iota(step_of_numbers[:], [[0, QT], [0, 4]], base=S, channel_multiplier=0).then_inc(start, 1)

        def one(b):
            Q.tensor_tensor(numbers, numbers, step_of_numbers[:], ALU.add).then_inc(tokens_ready, 1)
            pool.wait_ge(ve2_ready, b + 1)
            Q.tensor_tensor(rstd2[:], ve2[:], half[:], ALU.pow).then_inc(rstd2_ready, 1)
            wait_apart(pool, w, slots_ready, b + 1)
            pool.wait_ge(tokens_ready, b + 1)
            for n in range(QT):
                Q.indirect_dma_start(out=w["slots"], out_offset=bass.IndirectOffsetOnAxis(ap=r["slot"][:, n:n + 1], axis=0),
                                     in_=x2s[:, n, :], in_offset=None).then_inc(w["scattered"], 16)

        for_batches(pool, one, prepare)


def experts(nc, ctx, w, io):
    out = io["out"].rearrange("b s d -> (b s) d")
    NTOK, D = out.shape
    NT, NE, F = NTOK // P, w["gu"].shape[1], w["gu"].shape[2] // 2
    NS = NT + NE - 1
    FC = w["down"].shape[2]
    tail = F - (FC - 1) * P

    def sb(name, shape, dt=F32):
        return ctx.enter_context(nc.sbuf_tensor(name, shape, dt))

    def sem(name):
        return ctx.enter_context(nc.semaphore(name))

    expert, tile_at = w["list"]["expert"], w["list"]["tile_at"]
    RING = 4
    LEAD = 2 * RING
    xs = sb("xs", [P, NS, D + 4])
    x_turn = sb("x_turn", [P, RING, D])
    token = sb("token", [P, RING], U32)
    xsT = sb("xsT", [P, 2, P])
    silu = sb("silu", [P, 2, F])
    hid = sb("hid", [P, 2, FC * P])
    hidT = sb("hidT", [P, 2, FC, P])
    t3 = sb("t3", [P, 2, D])
    st3 = sb("st3", [P, 2, 6])
    mv3 = sb("mv3", [P, 2, 2])
    ve3 = sb("ve3", [P, 2])
    rstd3 = sb("rstd3", [P, 2])
    y3 = sb("y3", [P, RING, D])
    half3 = sb("half3", [P, 1])
    warm = sb("warm", [P, 1])
    psX = ctx.enter_context(nc.psum_tensor("psXs", [P, 512], F32))
    psG = ctx.enter_context(nc.psum_tensor("psG", [P, 2, 512], F32))
    psU = ctx.enter_context(nc.psum_tensor("psU", [P, 2, 512], F32))
    psH = ctx.enter_context(nc.psum_tensor("psH", [P, 512], F32))
    psY = ctx.enter_context(nc.psum_tensor("psYs", [P, 2, 512], F32))

    xs_in = [sem(f"tile_rows_in{n}") for n in range(RING)]
    token_ready = sem("token_ready")
    x_turn_in = [sem(f"tile_in{n}") for n in range(RING)]
    stored = [sem(f"rows_stored{n}") for n in range(RING)]
    xT_done, xT_taken, gu_done, silu_ready = (sem(n) for n in ("xs_turned", "xsT_ready", "gu_done", "silu_ready"))
    hid_ready, hT_done, hT_taken, y_done, t3_ready = (sem(n) for n in ("hid_ready", "hid_turned", "hidT_ready", "y_done", "t3_ready"))
    st3_ready, mv3_ready, ve3_ready, rstd3_ready, y3_ready = (
        sem(n) for n in ("st3_ready", "mv3_ready", "ve3_ready", "rstd3_ready", "y3_ready"))
    hid_cleared, half_set = sem("hid_cleared"), sem("half_set")
    c = w["route_consts"]
    block = ctx.enter_context(nc.Block())
    tile_rows = w["slots"].rearrange("(s p) c -> p s c", p=P)

    def pipeline(eng, one):
        loops = (NS - 1 - LEAD) // RING
        for s in range(LEAD):
            one(s, s % RING, s // RING)
        with eng.Fori(0, loops) as r:
            for m in range(RING):
                one(LEAD + m + RING * r, m, LEAD // RING + r)
        for s in range(LEAD + RING * loops, NS + 3):
            one(s, s % RING, s // RING)

    def place_of(m, h, back):
        return (m - back) % RING, h + (m - back) // RING

    def inside(s, back):
        return not isinstance(s, int) or 0 <= s - back < NS

    def of(tiles, s):
        return tiles[:, bass.ds(s, 1)].rearrange("p s c -> p (s c)")

    @block.vector
    def _(dve):
        V = nc.vector
        V.memset(hid[:], 0.0).then_inc(hid_cleared, 1)

        def one(s, m, h):
            p = m % 2
            if inside(s, 0):
                dve.wait_ge(silu_ready, s + 1)
                if inside(s, 2):
                    dve.wait_ge(hT_done, s - 1)
                V.tensor_tensor(hid[:, p, 0:F], silu[:, p, :], psU[:, p, 0:F], ALU.mult).then_inc(hid_ready, 1)
            if inside(s, 3):
                dve.wait_ge(rstd3_ready, s - 2)
                place, uses = place_of(m, h, 3)
                if inside(s, 3 + RING):
                    dve.wait_ge(stored[place], 16 * uses)
                V.tensor_scalar(y3[:, place], t3[:, 1 - p], mv3[:, 1 - p, 0:1], rstd3[:, 1 - p:2 - p],
                                ALU.subtract, ALU.mult).then_inc(y3_ready, 1)
            if inside(s, 2):
                dve.wait_ge(y_done, s - 1)
                place, uses = place_of(m, h, 2)
                dve.wait_ge(xs_in[place], 16 * (uses + 1))
                V.tensor_tensor(t3[:, p], psY[:, p, 0:D], of(xs, s - 2)[:, 0:D], ALU.add).then_inc(t3_ready, 1)
                dve.wait_ge(t3_ready, s - 1)
                V.bn_stats(st3[:, p], t3[:, p]).then_inc(st3_ready, 1)
                wait_apart(dve, w, st3_ready, s - 1)
                V.bn_aggr(mv3[:, p], st3[:, p]).then_inc(mv3_ready, 1)
                dve.wait_ge(mv3_ready, s - 1)
                V.tensor_scalar(ve3[:, p:p + 1], mv3[:, p, 1:2], LN_EPS, None, ALU.add).then_inc(ve3_ready, 1)

        pipeline(dve, one)

    @block.tensor
    def _(pe):
        def mm(out_, l, r, start=True, stop=True):
            return nc.tensor.matmul(out_, l, r, start=start, stop=stop)

        pe.wait_ge(w["background_in"], 16 * len(w["background"]))

        def turn(place, uses):
            pe.wait_ge(x_turn_in[place], 16 * (uses + 1))
            nc.tensor.transpose(psX[:, 0:P], x_turn[:, place, :], w["ident"]).then_inc(xT_done, 1)

        def one(s, m, h):
            p = m % 2
            if inside(s, 0):
                e = pe.snap(gu_expert, min_val=0, max_val=NE - 1)
                pe.wait_ge(xT_taken, s + 1)
                if inside(s, 2):
                    pe.wait_ge(hid_ready, s - 1)
                for n, bank in ((0, psG), (1, psU)):
                    last = mm(bank[:, p, 0:F], xsT[:, p, :], w["gu"][:, bass.ds(e, 1), n * F:(n + 1) * F].rearrange("k e n -> k (e n)"))
                last.then_inc(gu_done, 1)
            if inside(s, -1):
                turn(*place_of(m, h, -1))
                pe.reg_load(gu_expert, expert[0:1, bass.ds(s + 1, 1)])
            if inside(s, 2):
                e = pe.snap(down_expert, min_val=0, max_val=NE - 1)
                pe.wait_ge(hT_taken, s - 1)
                if inside(s, 4):
                    pe.wait_ge(t3_ready, s - 3)
                for n in range(FC):
                    k = P if n < FC - 1 else tail
                    last = mm(psY[:, p, 0:D], hidT[0:k, p, n, :], w["down"][0:k, bass.ds(e, 1), n, :].rearrange("k e n -> k (e n)"),
                              start=n == 0, stop=n == FC - 1)
                last.then_inc(y_done, 1)
            if inside(s, 1):
                pe.reg_load(down_expert, expert[0:1, bass.ds(s - 1, 1)])
            if inside(s, 1):
                pe.wait_ge(hid_ready, s)
                if inside(s, 2):
                    pe.wait_ge(hT_taken, s - 1)
                for n in range(FC):
                    last = nc.tensor.transpose(psH[:, n * P:(n + 1) * P], hid[:, 1 - p, n * P:(n + 1) * P], w["ident"])
                last.then_inc(hT_done, 1)

        gu_expert, down_expert = pe.alloc_register("gu_expert"), pe.alloc_register("down_expert")
        pe.reg_load(gu_expert, expert[0:1, 0:1])
        pe.wait_ge(hid_cleared, 1)
        turn(0, 0)
        pipeline(pe, one)

    @block.scalar
    def _(act):
        def turned(s, p):
            act.wait_ge(xT_done, s + 1)
            if inside(s, 2):
                act.wait_ge(gu_done, s - 1)
            nc.scalar.activation(xsT[:, p, :], psX[:, 0:P], ACT.Identity).then_inc(xT_taken, 1)

        def one(s, m, h):
            p = m % 2
            if inside(s, 0):
                act.wait_ge(gu_done, s + 1)
                if inside(s, 2):
                    act.wait_ge(hid_ready, s - 1)
                nc.scalar.activation(silu[:, p, :], psG[:, p, 0:F], ACT.Silu).then_inc(silu_ready, 1)
            if inside(s, -1):
                turned(s + 1, 1 - p)
            if inside(s, 1):
                act.wait_ge(hT_done, s)
                if inside(s, 3):
                    act.wait_ge(y_done, s - 2)
                nc.scalar.activation(hidT[:, 1 - p].rearrange("p n t -> p (n t)"), psH[:, 0:FC * P], ACT.Identity).then_inc(hT_taken, 1)

        nc.scalar.activation(warm[:], w["ident"][:, 0:1], ACT.Silu)
        turned(0, 0)
        pipeline(act, one)

    @block.sync
    def _(sp):
        sp.wait_ge(w["background_in"], 16 * len(w["background"]))

        def one(s, m, h):
            p = m % 2
            if inside(s, 0):
                tile = sp.value_load(tile_at[0:1, bass.ds(s, 1)], min_val=0, max_val=NE * (NT + 1))
                if inside(s, RING):
                    sp.wait_ge(xT_done, s - RING + 1)
                sp.dma_start(x_turn[:, m], of(tile_rows, tile)[:, 0:D]).then_inc(x_turn_in[m], 16)
                if inside(s, RING):
                    sp.wait_ge(xs_in[m], 16 * h)
                sp.dma_start(of(xs, s), of(tile_rows, tile)).then_inc(xs_in[m], 16)

        pipeline(sp, one)

    @block.gpsimd
    def _(pool):
        nc.gpsimd.memset(half3[:], -0.5).then_inc(half_set, 1)
        pool.wait_ge(half_set, 1)
        def one(s, m, h):
            p = m % 2
            if inside(s, 2):
                pool.wait_ge(ve3_ready, s - 1)
                nc.gpsimd.tensor_tensor(rstd3[:, p:p + 1], ve3[:, p:p + 1], half3[:], ALU.pow).then_inc(rstd3_ready, 1)
            if inside(s, 3):
                Q = nc.gpsimd
                place, uses = place_of(m, h, 3)
                if inside(s, 3 + RING):
                    pool.wait_ge(stored[place], 16 * uses)
                Q.tensor_copy(token[:, place:place + 1], of(xs, s - 3)[:, D:D + 1].bitcast(U32)).then_inc(token_ready, 1)
                wait_apart(pool, w, token_ready, s - 2)
                pool.wait_ge(y3_ready, s - 2)
                Q.indirect_dma_start(out=out, out_offset=bass.IndirectOffsetOnAxis(ap=token[:, place:place + 1], axis=0),
                                     in_=y3[:, place, :], in_offset=None, bounds_check=NTOK - 1,
                                     oob_is_err=False).then_inc(stored[place], 16)

        pipeline(pool, one)
        for n in range(RING):
            pool.wait_ge(stored[n], 16 * ((NS + RING - 1 - n) // RING))


def decoder_layer(nc, x, xT, ctxT, first_weights, weights, bias_rows, gate_up, down, out):
    B, S, D = x.shape
    NT = B * S // P
    NE, F = down.shape[0], down.shape[1]
    NS = NT + NE - 1
    io = {"x": x, "xT": xT, "ctxT": ctxT, "out": out}
    with ExitStack() as whole:
        def sb(name, shape, dt=F32):
            return whole.enter_context(nc.sbuf_tensor(name, shape, dt))

        w = {"heads": sb("heads", [P, P], F32R)}
        route = {}

        def columns(tile, parts_):
            at = 0
            for into, name, n in parts_:
                into[name] = tile[:, at:at + n]
                at += n
            assert at == tile.shape[1]

        first_sb = sb("first_weights_sb", [P, first_weights.shape[1]])
        weights_sb = sb("weights_sb", [P, weights.shape[1]])
        rows_sb = sb("bias_rows_sb", [P, bias_rows.shape[0]])
        columns(first_sb, [(w, "wq1", D), (w, "wk1", D), (w, "bcol", 5), (w, "ident", P)])
        columns(weights_sb, [(w, n, D) for n in ("wv1T", "wo1", "wq2", "wk2", "wv2", "wo2")]
                + [(w, "router", NE), (w, "same_head", P), (w, "place", J), (route, "earlier", P), (route, "ones", P),
                   (route, "region", NE), (route, "region_tile", NE), (route, "rank", NE), (route, "ones8", NE), (route, "steps", NT), (route, "tile", NS)])
        columns(rows_sb, [(w, "bo1", D), (w, "bv2", D), (w, "bo2", D)])
        w["route_consts"] = route
        w["qnorm"], w["knorm"] = sb("qnorm", [P, B]), sb("knorm", [P, B])
        w["x1b"] = sb("x1b", [P, B, S // P, D])
        w["x1T"] = sb("x1T", [P, B, S])
        w["counting"] = sb("counting", [P, 2, P], BF16)
        w["list"] = list_buffers(sb, NE, NT)
        w["next_slot"] = sb("next_slot", [P, NE])
        w["scattered"] = whole.enter_context(nc.semaphore("rows_scattered"))
        w["empty"] = sb("empty", [P, D + 4])
        w["gu"] = sb("gu", [P, NE, 2 * F])
        w["down"] = sb("down_sb", [P, NE, -(-F // P), D])
        w["slots"] = nc.dram_tensor("slots", [(NE * (NT + 1) + 1) * P, D + 4], F32).ap()
        w["first_loads"] = [(first_sb[:], first_weights)]
        w["loads"] = [(weights_sb[:], weights),
                      (rows_sb[:], bias_rows.rearrange("(a n) -> a n", a=1).broadcast_to([P, bias_rows.shape[0]]))]
        w["n"] = 16 * len(w["loads"])
        w["unbounded"] = sb("unbounded", [1, 1], I32)
        w["decided"] = whole.enter_context(nc.semaphore("decided"))
        w["first_in"] = whole.enter_context(nc.semaphore("first_weights_in"))
        whole_tiles = F // P * P
        w["background"] = [(w["gu"][:], gate_up)]
        w["background"] += [(w["down"][:, :, n, :], down[:, n * P:(n + 1) * P, :].rearrange("e k n -> k e n")) for n in range(F // P)]
        w["background"] += [(w["down"][0:F - whole_tiles, :, F // P, :], down[:, whole_tiles:, :].rearrange("e k n -> k e n")),
                            (w["slots"][NE * (NT + 1) * P:], w["empty"][:])]
        w["sem"] = whole.enter_context(nc.semaphore("weights_in"))
        w["background_in"] = whole.enter_context(nc.semaphore("background_in"))
        w["empty_ready"] = whole.enter_context(nc.semaphore("empty_ready"))
        with ExitStack() as ctx:
            attention(nc, ctx, w, io)
        with ExitStack() as ctx:
            exact_attention(nc, ctx, w, io)
        with ExitStack() as ctx:
            experts(nc, ctx, w, io)


def _laid_out(x, ctx_1024, **inputs):
    import numpy as np

    plain = np.ascontiguousarray
    B, S, D = x.shape
    NE, F, _ = inputs["L0_ffn_gate_w"].shape
    NT = B * S // P
    out = {"x": plain(x), "xT": plain(x.reshape(B * S, D).T), "ctxT": plain(ctx_1024.reshape(-1, D).T)}
    W = lambda layer, n: inputs[f"L0_{layer}_W{n}"]
    b = lambda layer, n: inputs[f"L0_{layer}_b{n}"]
    gate_up = np.concatenate([inputs["L0_ffn_gate_w"], inputs["L0_ffn_up_w"]], axis=1)
    out["gate_up"] = plain(gate_up.transpose(2, 0, 1))
    out["down"] = plain(inputs["L0_ffn_down_w"].transpose(0, 2, 1))
    p = np.arange(P)
    f32 = lambda *a: [x.astype(np.float32) for x in a]
    out["first_weights"] = np.concatenate(
        [W("attn", "q"), W("attn", "k")]
        + [b(*n)[:, None] for n in (("attn", "q"), ("attn", "k"), ("xattn", "q"), ("xattn", "k"), ("attn", "v"))]
        + f32(np.eye(P)), axis=1)
    out["weights"] = np.concatenate(
        [W("attn", "v").T, W("attn", "o"), W("xattn", "q"), W("xattn", "k"), W("xattn", "v"),
         W("xattn", "o").reshape(H, E, D).transpose(1, 0, 2).reshape(D, D),
         inputs["L0_ffn_router_w"].T]
        + f32(p[:, None] // E == p[None, :] // E,
              p[:, None] % 32 // E == np.arange(J)[None, :],
              p[:, None] < p[None, :],
              np.ones((P, P)),
              np.tile(np.arange(NE) * (NT + 1) * P, (P, 1)),
              np.tile(np.arange(NE) * (NT + 1), (P, 1)),
              np.tile(np.arange(NE, 0, -1), (P, 1)),
              np.ones((P, NE)),
              np.tile(np.arange(NT) * P, (P, 1)),
              np.tile(np.arange(NT + NE - 1), (P, 1))), axis=1)
    out["bias_rows"] = np.concatenate([b("attn", "o"), b("xattn", "v"), b("xattn", "o")])
    return out


def kernel(**inputs):
    import numpy as np
    import concourse.bacc as bacc
    from concourse.bass_utils import run_bass_kernel_spmd

    nc = bacc.Bacc("TRN2", target_bir_lowering=False, num_devices=1)
    arrays = _laid_out(**{k: np.asarray(v) for k, v in inputs.items()})
    args = {n: nc.dram_tensor(n, a.shape, mybir.dt.from_np(a.dtype), kind="ExternalInput").ap() for n, a in arrays.items()}
    shape = inputs["x"].shape
    out = nc.dram_tensor("out", shape, F32, kind="ExternalOutput").ap()
    decoder_layer(nc, out=out, **args)
    r = run_bass_kernel_spmd(nc, [arrays], core_ids=[0])
    return r.results[0]["out"]
```
